# Optimizing a Trainium2 kernel written in Bass

```python
import numpy as np
import jax
import jax.numpy as jnp

def _softmax(x, axis=-1):
    return jax.nn.softmax(x, axis=axis)

def _gelu(x):
    return jax.nn.gelu(x, approximate=True)

def _silu(x):
    return jax.nn.silu(x)

def _sigmoid(x):
    return jax.nn.sigmoid(x)

def _layernorm(x, axis=-1, eps=1e-05):
    m = jnp.mean(x, axis=axis, keepdims=True)
    v = jnp.var(x, axis=axis, keepdims=True)
    return (x - m) / jnp.sqrt(v + eps)

def _scatter_add(tgt, idx, src, axis=0):
    return tgt.at[idx].add(src)

def _segment_sum(src, seg, n):
    return jax.ops.segment_sum(src, seg, n)
kernel_name = 'mk_gnn_preln_d1_gnn_r8_bfe1f3'

def setup_inputs(seed: int=0):
    np.random.seed(seed)
    _w = jnp.asarray

    def _rec_inputs():
        import jax
        import jax.numpy as jnp
        _gk = jax.random.key(seed)
        x = -0.000202 + 1 * jax.random.normal(jax.random.fold_in(_gk, 1), (6250, 128), jnp.float32)
        src = jax.random.randint(jax.random.fold_in(_gk, 2), (100000,), 0, 6250, jnp.int32)
        dst = jax.random.randint(jax.random.fold_in(_gk, 3), (100000,), 0, 6250, jnp.int32)
        _o = jnp.argsort(dst, stable=True)
        src = src[_o]
        dst = dst[_o]
        edge_attr_64 = 0.000189758 + 1.00013 * jax.random.normal(jax.random.fold_in(_gk, 11), (100000, 64), jnp.float32)
        return (x, src, dst, edge_attr_64)
    x, src, dst, edge_attr_64 = _rec_inputs()

    def _L0_gnn_setup():
        import jax, jax.numpy as jnp
        import numpy as np
        NODE_DIM, EDGE_DIM, OUT_DIM = (128, 64, 128)
        N_NODES, N_EDGES = (6250, 100000)
        key = jax.random.key(seed)
        ks = jax.random.split(key, 12)
        x = jax.random.normal(ks[0], (N_NODES, NODE_DIM), dtype=jnp.float32)
        edge_index = jax.random.randint(ks[1], (2, N_EDGES), 0, N_NODES, dtype=jnp.int64)
        edge_attr = jax.random.normal(ks[2], (N_EDGES, EDGE_DIM), dtype=jnp.float32)
        s = 0.05
        W1 = jax.random.normal(ks[3], (NODE_DIM + EDGE_DIM, OUT_DIM), dtype=jnp.float32) * s
        b1 = jnp.zeros((OUT_DIM,), dtype=jnp.float32)
        W2 = jax.random.normal(ks[4], (OUT_DIM, OUT_DIM), dtype=jnp.float32) * s
        b2 = jnp.zeros((OUT_DIM,), dtype=jnp.float32)
        Wm = jax.random.normal(ks[5], (OUT_DIM, OUT_DIM), dtype=jnp.float32) * s
        bm = jnp.zeros((OUT_DIM,), dtype=jnp.float32)
        Wx = jax.random.normal(ks[6], (OUT_DIM, OUT_DIM), dtype=jnp.float32) * s
        bx = jnp.zeros((OUT_DIM,), dtype=jnp.float32)
        Ws = jax.random.normal(ks[7], (OUT_DIM, OUT_DIM), dtype=jnp.float32) * s
        bs = jnp.zeros((OUT_DIM,), dtype=jnp.float32)
        return {'x': x, 'edge_index': edge_index, 'edge_attr': edge_attr, 'W1': W1, 'b1': b1, 'W2': W2, 'b2': b2, 'Wm': Wm, 'bm': bm, 'Wx': Wx, 'bx': bx, 'Ws': Ws, 'bs': bs}
    _L0_gnn_all = _L0_gnn_setup()
    _L0_gnn_in = {k: v for k, v in _L0_gnn_all.items() if k in ('W1', 'b1', 'W2', 'b2', 'Wm', 'bm', 'Wx', 'bx', 'Ws', 'bs')}
    del _L0_gnn_all
    return {'x': x, 'src': src, 'dst': dst, 'edge_attr_64': edge_attr_64, 'L0_gnn_W1': _L0_gnn_in['W1'], 'L0_gnn_b1': _L0_gnn_in['b1'], 'L0_gnn_W2': _L0_gnn_in['W2'], 'L0_gnn_b2': _L0_gnn_in['b2'], 'L0_gnn_Wm': _L0_gnn_in['Wm'], 'L0_gnn_bm': _L0_gnn_in['bm'], 'L0_gnn_Wx': _L0_gnn_in['Wx'], 'L0_gnn_bx': _L0_gnn_in['bx'], 'L0_gnn_Ws': _L0_gnn_in['Ws'], 'L0_gnn_bs': _L0_gnn_in['bs']}

def reference(x, src, dst, edge_attr_64, L0_gnn_W1, L0_gnn_b1, L0_gnn_W2, L0_gnn_b2, L0_gnn_Wm, L0_gnn_bm, L0_gnn_Wx, L0_gnn_bx, L0_gnn_Ws, L0_gnn_bs):
    import jax
    import jax.numpy as jnp

    def _L0_gnn_ref(x, edge_index, edge_attr, W1, b1, W2, b2, Wm, bm, Wx, bx, Ws, bs):
        import jax, jax.numpy as jnp
        import numpy as np
        NODE_DIM, EDGE_DIM, OUT_DIM = (128, 64, 128)
        N_NODES, N_EDGES = (6250, 100000)
        num_nodes = x.shape[0]
        src, dst = (edge_index[0], edge_index[1])
        combined = jnp.concatenate([x[dst], edge_attr], axis=-1)
        messages = jax.nn.relu(combined @ W1 + b1) @ W2 + b2
        agg_sum = jax.ops.segment_sum(messages, dst, num_segments=num_nodes)
        count = jax.ops.segment_sum(jnp.ones((messages.shape[0],), dtype=messages.dtype), dst, num_segments=num_nodes)
        agg_mean = agg_sum / jnp.maximum(count, 1.0)[:, None]
        agg_max = jax.ops.segment_max(messages, dst, num_segments=num_nodes)
        agg_max = jnp.where(jnp.isneginf(agg_max), 0.0, agg_max)
        out = agg_mean @ Wm + bm + (agg_max @ Wx + bx) + (agg_sum @ Ws + bs)
        return out
    edge_index = jnp.stack([src, dst])
    h = jnp.maximum(_layernorm(x, axis=-1), 0.0)
    x = x + _L0_gnn_ref(h, edge_index, edge_attr_64, L0_gnn_W1, L0_gnn_b1, L0_gnn_W2, L0_gnn_b2, L0_gnn_Wm, L0_gnn_bm, L0_gnn_Wx, L0_gnn_bx, L0_gnn_Ws, L0_gnn_bs)
    return x

_drawn_inputs = setup_inputs


def setup_inputs(seed=0):
    import zlib

    import numpy as np

    out = dict(_drawn_inputs(seed))
    spreads = {'L0_gnn_b1': (0.0, 0.1),
     'L0_gnn_b2': (0.0, 0.1),
     'L0_gnn_bm': (0.0, 0.1),
     'L0_gnn_bx': (0.0, 0.1),
     'L0_gnn_bs': (0.0, 0.1)}
    factors = {}
    for name, (base, spread) in spreads.items():
        noise = np.random.default_rng([zlib.crc32(name.encode()), seed]).standard_normal(out[name].shape)
        drawn = base * np.exp(spread * noise) if base else spread * noise
        out[name] = jnp.asarray(drawn.astype(out[name].dtype))
    for name, factor in factors.items():
        out[name] = (out[name] * factor).astype(out[name].dtype)
    return out
```

```python
from contextlib import ExitStack

import concourse.bass as bass
from concourse import mybir

F32 = mybir.dt.float32
BF16 = mybir.dt.bfloat16
I32 = mybir.dt.int32
ALU = mybir.AluOpType
ACT = mybir.ActivationFunctionType
AX = mybir.AxisListType

P = 128
BIG = 1e30
EPS = 1e-5


def at_least(engine, semaphore, value, alone=False):
    if isinstance(value, int) and value <= 0:
        return
    engine.wait_ge(semaphore, value)
    if alone:
        engine.nop(nofuse=True)


def rolled(engine, n, order):
    least, most = min(o for _, o in order), max(o for _, o in order)
    first = -least + (-least) % 2 + 2
    last = n - most
    last -= (last - first) % 2

    def at(t):
        for step, o in order:
            if 0 <= t + o < n:
                step((t + o) // 2, (t + o) % 2)
    for t in range(-most, first):
        at(t)
    with engine.Fori(first // 2, last // 2) as i:
        for k in range(2):
            for step, o in order:
                step(i + (k + o) // 2, (k + o) % 2)
    for t in range(last, n - least):
        at(t)


def gnn_kernel(nc, x, dst, edge, W1, b1, W2, b2, Wm, bm, Wx, bx, Ws, bs, out):
    N, F = x.shape
    E, FE = edge.shape
    assert F == P and 2 * FE == P
    L = 4
    NPP = -(-N // P)
    FULL = N // NPP
    REST = N - FULL * NPP
    EVEN = FULL // 16 * 16
    CHUNKS = E // L
    T = -(-(CHUNKS + NPP * P) // P)
    BS = 250
    NB = E // BS
    assert FULL == P - 1 and E % BS == 0 and E % L == 0 and T < 256 and T % 2

    utab = nc.dram_tensor("utab", (NPP * P, F + 2), F32, kind="Internal").ap()
    rtab = nc.dram_tensor("rtab", (T * P, 2 * F), F32, kind="Internal").ap()
    chunk_rows = edge.rearrange("(c l) f -> c (l f)", l=L)
    search_rows = dst.rearrange("(a b) -> a b", b=BS)

    def node_rows(a):
        whole = a[0:FULL * NPP, :].rearrange("(p b) f -> p b f", b=NPP)
        return ((0, EVEN, NPP, whole[0:EVEN]), (EVEN, FULL, NPP, whole[EVEN:FULL]),
                (FULL, FULL + 1, REST, a[FULL * NPP:N, :].rearrange("(p b) f -> p b f", b=REST)))

    with ExitStack() as ctx:
        def sb(name, shape, dt=F32):
            return ctx.enter_context(nc.sbuf_tensor(name, shape, dt))

        def sem(name):
            return ctx.enter_context(nc.semaphore(name))

        bank = [ctx.enter_context(nc.psum_tensor(f"bank{i}", [P, 512], F32)) for i in range(8)]
        ps_z, ps_m, ps_t, ps_mask, ps_r = bank[0:2], bank[2:4], bank[4:6], bank[6], bank[7]

        ident = sb("ident", [P, P])
        identb = sb("identb", [P, P], BF16)
        neg_ident = sb("neg_ident", [P, P], BF16)
        onesb = sb("onesb", [P, P], BF16)
        onesf = sb("onesf", [1, P])
        tri = sb("tri", [P, P], BF16)
        iota_i = sb("iota_i", [P, 256], I32)
        iotab = sb("iotab", [P, 256], BF16)
        w1a = sb("w1a", [P, F])
        w1b = sb("w1b", [P, 2, F])
        w2 = sb("w2", [P, F])
        wm = sb("wm", [P, F])
        wx = sb("wx", [P, F])
        ws = sb("ws", [P, F])
        b1r = sb("b1r", [P, F])
        b2r = sb("b2r", [P, F])
        bor = sb("bor", [P, 3, F])
        xs = sb("xs", [P, NPP, F])
        us = sb("us", [P, NPP, F + 2])
        nodei = sb("nodei", [P, NPP + 1], I32)
        nodef = sb("nodef", [P, NPP + 1])
        stats = sb("stats", [P, NPP, 6])
        mv = sb("mv", [P, NPP, 2])
        sd = sb("sd", [P, 4, NPP])
        rstd = sb("rstd", [P, NPP])
        coarse = sb("coarse", [P, NPP + 1])
        coarsei = sb("coarsei", [P, NPP + 1], I32)
        fine = sb("fine", [P, NPP + 1])
        start = sb("start", [P, NPP + 1])
        count = sb("count", [P, NPP])
        rcount = sb("rcount", [P, NPP])
        some = sb("some", [P, NPP])
        wi = sb("wi", [P, 4, NPP], I32)
        wf = sb("wf", [P, 4, NPP])
        goff = sb("goff", [P, NPP])
        gend = sb("gend", [P, NPP])
        gendi = sb("gendi", [P, NPP], I32)
        slots_l = sb("slots_l", [P, NPP])
        slotf = sb("slotf", [P, T])
        sloti = sb("sloti", [P, T], I32)
        starts = sb("starts", [P, T], BF16)
        goes_on = sb("goes_on", [P, T], BF16)
        total = sb("total", [P, T])
        zeros = sb("zeros", [P, T])
        upto = sb("upto", [P, T])
        s_node = sb("s_node", [P, T])
        s_chunk = sb("s_chunk", [P, T])
        s_index = sb("s_index", [P, T, 2], I32)
        s_edge = sb("s_edge", [P, T, L])
        last_i = sb("last_i", [1, NB], I32)
        last_f = sb("last_f", [1, NB])
        lasts = sb("lasts", [P, NB])
        found = sb("found", [P, NPP + 1, BS], I32)
        junk = sb("junk", [P, 2, NB])
        oh_lo = sb("oh_lo", [P, 2, P], BF16)
        oh_hi = sb("oh_hi", [P, 2, T], BF16)
        hn = sb("hn", [P, 2, F])
        hT = sb("hT", [P, 2, F])
        idx = sb("idx", [P, 2, 2], I32)
        ea = sb("ea", [P, 2, L * FE])
        ug = sb("ug", [P, 2, F + 2])
        eaT = sb("eaT", [P, 2, L // 2, P])
        nuT = sb("nuT", [P, 2, P])
        past = sb("past", [P, 2, L])
        inv = sb("inv", [P, 2, L], BF16)
        rp = sb("rp", [P, 2, L, P])
        half = sb("half", [P, 2, 2, P])
        rsum = sb("rsum", [P, 2, P])
        mred = sb("mred", [P, 2, P])
        smax = sb("smax", [P, 2, P])
        ssum = sb("ssum", [P, 2, P])
        rT = sb("rT", [P, 2, 2 * P])
        rg = sb("rg", [P, 2, 2 * F])
        ridx = sb("ridx", [P, 2, 1], I32)
        su = sb("su", [P, 2, 2, F])
        suT = sb("suT", [P, 2, 2, P])
        ag = sb("ag", [P, 2, 2, F])
        agT = sb("agT", [P, 2, 2, P])
        am = sb("am", [P, 2, 2, F])
        ob = sb("ob", [P, 2, F])

        x_in = sem("x_in")
        w_in = sem("w_in")
        last_in = sem("last_in")
        const_done = sem("const_done")
        pool_chain = sem("pool_chain")
        dve_chain = sem("dve_chain")
        lasts_bc = sem("lasts_bc")
        coarse_done = sem("coarse_done")
        coarse_step = sem("coarse_step")
        fine_step = sem("fine_step")
        stats_done = sem("stats_done")
        lasts_ready = sem("lasts_ready")
        found_in = sem("found_in")
        var_done = sem("var_done")
        sd_done = sem("sd_done")
        h_done = sem("h_done")
        h_turned = sem("h_turned")
        hT_done = sem("hT_done")
        u_done = sem("u_done")
        u_read = sem("u_read")
        oh_done = sem("oh_done")
        oh_used = sem("oh_used")
        hist_read = sem("hist_read")
        prefix_done = sem("prefix_done")
        edges_done = sem("edges_done")
        utab_out = sem("utab_out")
        chain = [0]

        def link(dve, instruction):
            chain[0] += 1
            instruction.then_inc(dve_chain, 1)
            dve.wait_ge(dve_chain, chain[0])

        X_DMAS = 3
        with nc.Block() as block:
            @block.sync
            def _(sp):
                sp.dma_start(last_i[:, :], search_rows[:, BS - 1:BS].rearrange("a b -> b a"),
                             allow_slow_non_contiguous=True).then_inc(last_in, 16)
                sp.wait_ge(const_done, 1)
                for p0, p1, nb, rows in node_rows(x):
                    sp.dma_start(xs[p0:p1, 0:nb, :], rows).then_inc(x_in, 16)
                sp.wait_ge(edges_done, 1)
                sp.dma_start(utab.rearrange("(p b) f -> p b f", b=NPP), us[:, :, :]).then_inc(utab_out, 16)
                sp.wait_ge(utab_out, 16)

            @block.scalar
            def _(act):
                act.dma_start(w1a[:, :], W1[0:F, :]).then_inc(w_in, 16)
                act.wait_ge(const_done, 1)
                act.dma_start(w1b[0:FE, 0, :], W1[F:F + FE, :]).then_inc(w_in, 16)
                act.dma_start(w1b[FE:P, 1, :], W1[F:F + FE, :]).then_inc(w_in, 16)
                for t, a in ((w2, W2), (wm, Wm), (wx, Wx), (ws, Ws)):
                    act.dma_start(t[:, :], a).then_inc(w_in, 16)
                for t, a in ((b1r[:, :], b1), (b2r[:, :], b2), (bor[:, 0, :], bm), (bor[:, 1, :], bx),
                             (bor[:, 2, :], bs)):
                    act.dma_start(t, a.rearrange("(a f) -> a f", a=1).broadcast_to([P, F])).then_inc(w_in, 16)
                act.wait_ge(var_done, 1)
                nc.scalar.activation(sd[:, 0, :], sd[:, 1, :], ACT.Sqrt).then_inc(sd_done, 1)

                def relu_h(i, k):
                    at_least(act, h_turned, 2 * i + k + 1)
                    at_least(act, u_done, 2 * i + k - 1)
                    nc.scalar.activation(hT[:, k, :], ps_t[k][:, 0:F], ACT.Relu).then_inc(hT_done, 1)
                rolled(act, NPP, [(relu_h, 0)])

            @block.gpsimd
            def _(pool):
                nc.gpsimd.memset(xs[:, REST:NPP, :], 0.0)
                nc.gpsimd.memset(w1b[:, :, :], 0.0).then_inc(const_done, 1)
                nc.gpsimd.iota(nodei[:, :], pattern=[[1, NPP + 1]], base=0, channel_multiplier=NPP)
                nc.gpsimd.iota(iota_i[:, :], pattern=[[1, 256]], base=0, channel_multiplier=0)
                nc.gpsimd.iota(sloti[:, :], pattern=[[P, T]], base=0, channel_multiplier=1)
                nc.gpsimd.memset(ident[:, :], 0.0)
                nc.gpsimd.memset(identb[:, :], 0.0)
                nc.gpsimd.memset(neg_ident[:, :], 0.0)
                nc.gpsimd.memset(onesb[:, :], 1.0)
                nc.gpsimd.memset(onesf[:, :], 1.0)
                nc.gpsimd.memset(zeros[:, :], 0.0)
                nc.gpsimd.memset(tri[:, :], 1.0).then_inc(pool_chain, 1)
                pool.wait_ge(pool_chain, 1)
                for m, v in ((ident, 1.0), (identb, 1.0), (neg_ident, -BIG)):
                    nc.gpsimd.affine_select(out=m[:, :], in_=m[:, :], compare_op=ALU.not_equal, fill=v, base=0,
                                            pattern=[[-1, P]], channel_multiplier=1)
                nc.gpsimd.affine_select(out=tri[:, :], in_=tri[:, :], compare_op=ALU.is_ge, fill=0.0, base=0,
                                        pattern=[[1, P]], channel_multiplier=-1).then_inc(const_done, 1)
                pool.wait_ge(coarse_done, 1)
                for b in range(NPP + 1):
                    pool.indirect_dma_start(
                        out=found[:, b, :], out_offset=None, in_=search_rows,
                        in_offset=bass.IndirectOffsetOnAxis(ap=coarsei[:, b:b + 1], axis=0)).then_inc(found_in, 16)

            @block.tensor
            def _(pe):
                pe.wait_ge(const_done, 2)
                pe.wait_ge(lasts_ready, 1)
                nc.tensor.matmul(ps_z[0][:, 0:NB], onesf[0:1, :], last_f[0:1, :], start=True,
                                 stop=True).then_inc(lasts_bc, 1)
                pe.wait_ge(w_in, 16 * 12)

                def u_product(i, k):
                    at_least(pe, h_done, 2 * i + k + 1)
                    nc.tensor.transpose(ps_t[k][:, 0:F], hn[:, k, :], ident[:, :]).then_inc(h_turned, 1)
                    at_least(pe, hT_done, 2 * i + k + 1)
                    at_least(pe, u_read, 2 * i + k - 1)
                    nc.tensor.matmul(ps_m[k][:, 0:F], hT[:, k, :], w1a[:, :], start=True,
                                     stop=True).then_inc(u_done, 1)
                rolled(pe, NPP, [(u_product, 0)])

                def add_nodes(i, k):
                    b = 2 * i + k
                    at_least(pe, oh_done, b + 1)
                    is_int = isinstance(b, int)
                    nc.tensor.matmul(ps_mask[:, 0:T], oh_lo[:, k, :], oh_hi[:, k, :], start=is_int and b == 0,
                                     stop=is_int and b == NPP - 1).then_inc(oh_used, 1)
                rolled(pe, NPP, [(add_nodes, 0)])
                pe.wait_ge(hist_read, 1)
                nc.tensor.matmul(ps_r[:, 0:T], tri[:, :], starts[:, :], start=True, stop=True)
                nc.tensor.matmul(ps_r[:, 256:256 + T], onesb[:, :], starts[:, :], start=True,
                                 stop=True).then_inc(prefix_done, 1)

            @block.vector
            def _(dve):
                v = nc.vector
                dve.wait_ge(const_done, 2)
                v.tensor_copy(iotab[:, :], iota_i[:, :])
                v.tensor_copy(nodef[:, :], nodei[:, :])
                v.tensor_copy(slotf[:, :], sloti[:, :])
                dve.wait_ge(last_in, 16)
                v.tensor_copy(last_f[:, :], last_i[:, :]).then_inc(lasts_ready, 1)
                dve.wait_ge(lasts_bc, 1)
                link(dve, v.tensor_copy(lasts[:, :], ps_z[0][:, 0:NB]))
                def count_blocks(i, k):
                    b = 2 * i + k
                    at_least(dve, coarse_step, b - 1)
                    v.tensor_scalar(junk[:, k, :], lasts[:, :], nodef[:, bass.ds(b, 1)], 0.0, ALU.is_lt, ALU.add,
                                    accum_out=coarse[:, bass.ds(b, 1)]).then_inc(coarse_step, 1)
                rolled(dve, NPP + 1, [(count_blocks, 0)])
                dve.wait_ge(coarse_step, NPP + 1)
                link(dve, v.tensor_scalar(coarse[:, :], coarse[:, :], float(NB - 1), None, ALU.min))
                v.tensor_copy(coarsei[:, :], coarse[:, :]).then_inc(coarse_done, 1)

                dve.wait_ge(x_in, 16 * X_DMAS)
                def row_stats(i, k):
                    b = bass.ds(2 * i + k, 1)
                    v.bn_stats(stats[:, b, :], xs[:, b, :]).then_inc(stats_done, 1)
                rolled(dve, NPP, [(row_stats, 0)])
                dve.wait_ge(stats_done, NPP)
                for b in range(NPP):
                    last = v.bn_aggr(mv[:, b, :], stats[:, b, :])
                link(dve, last)
                v.tensor_scalar(sd[:, 1, :], mv[:, :, 1], EPS, None, ALU.add).then_inc(var_done, 1)
                dve.wait_ge(sd_done, 1)
                link(dve, v.reciprocal(sd[:, 2, :], sd[:, 0, :]))
                link(dve, v.tensor_tensor(sd[:, 3, :], sd[:, 1, :], sd[:, 2, :], ALU.mult))
                link(dve, v.tensor_tensor(sd[:, 2, :], sd[:, 3, :], sd[:, 0, :], ALU.add))
                link(dve, v.tensor_scalar(sd[:, 3, :], sd[:, 2, :], 0.5, None, ALU.mult))
                link(dve, v.reciprocal(rstd[:, :], sd[:, 3, :]))
                dve.wait_ge(w_in, 16 * 12)

                def normalise(i, k):
                    b = 2 * i + k
                    at_least(dve, h_turned, b - 1)
                    v.tensor_scalar(hn[:, k, :], xs[:, bass.ds(b, 1), :], mv[:, bass.ds(b, 1), 0],
                                    rstd[:, bass.ds(b, 1)], ALU.subtract, ALU.mult).then_inc(h_done, 1)

                def add_b1(i, k):
                    at_least(dve, u_done, 2 * i + k + 1)
                    v.tensor_tensor(us[:, bass.ds(2 * i + k, 1), 0:F], ps_m[k][:, 0:F], b1r[:, :],
                                    ALU.add).then_inc(u_read, 1)

                rolled(dve, NPP, [(normalise, 0), (add_b1, -1)])

                dve.wait_ge(found_in, 16 * (NPP + 1))
                def count_edges(i, k):
                    b = 2 * i + k
                    at_least(dve, fine_step, b - 1)
                    v.tensor_scalar(junk[:, k, 0:BS], found[:, bass.ds(b, 1), :], nodef[:, bass.ds(b, 1)], 0.0,
                                    ALU.is_lt, ALU.add, accum_out=fine[:, bass.ds(b, 1)]).then_inc(fine_step, 1)
                rolled(dve, NPP + 1, [(count_edges, 0)])
                dve.wait_ge(fine_step, NPP + 1)
                link(dve, v.scalar_tensor_tensor(start[:, :], coarse[:, :], float(BS), fine[:, :], ALU.mult,
                                                 ALU.add))
                first, end = start[:, 0:NPP], start[:, 1:NPP + 1]
                v.tensor_copy(us[:, :, F], first)
                v.tensor_copy(us[:, :, F + 1], end).then_inc(edges_done, 1)
                v.tensor_copy(wi[:, 0, :], first)
                v.scalar_tensor_tensor(wf[:, 0, :], end, -1.0, first, ALU.add, ALU.max)
                link(dve, v.tensor_tensor(count[:, :], end, first, ALU.subtract))
                v.tensor_copy(wi[:, 1, :], wf[:, 0, :])
                v.tensor_scalar(wf[:, 1, :], count[:, :], 1.0, None, ALU.max)
                link(dve, v.tensor_scalar(some[:, :], count[:, :], 0.0, None, ALU.is_gt))
                v.reciprocal(rcount[:, :], wf[:, 1, :])
                shift = (L - 1).bit_length()
                link(dve, v.tensor_scalar(wi[:, 2:4, :], wi[:, 0:2, :], shift, None, ALU.logical_shift_right))
                link(dve, v.tensor_copy(wf[:, 2:4, :], wi[:, 2:4, :]))
                v.tensor_tensor(goff[:, :], wf[:, 2, :], nodef[:, 0:NPP], ALU.add)
                link(dve, v.tensor_tensor(gend[:, :], wf[:, 3, :], nodef[:, 0:NPP], ALU.add))
                v.tensor_copy(gendi[:, :], gend[:, :])
                v.tensor_copy(wi[:, 0, :], goff[:, :])
                link(dve, v.tensor_tensor(slots_l[:, :], gend[:, :], goff[:, :], ALU.subtract))
                v.tensor_scalar(slots_l[:, :], slots_l[:, :], 1.0, float(L), ALU.add, ALU.mult)
                v.tensor_scalar(wi[:, 1, :], wi[:, 0, :], 7, None, ALU.logical_shift_right)
                link(dve, v.tensor_scalar(wi[:, 2, :], wi[:, 0, :], P - 1, None, ALU.bitwise_and))
                link(dve, v.tensor_copy(wf[:, 1:3, :], wi[:, 1:3, :]))

                def one_hots(i, k):
                    b = bass.ds(2 * i + k, 1)
                    at_least(dve, oh_used, 2 * i + k - 1)
                    v.tensor_scalar(oh_lo[:, k, :], iotab[:, 0:P], wf[:, 2, b], None, ALU.is_equal)
                    v.tensor_scalar(oh_hi[:, k, :], iotab[:, 0:T], wf[:, 1, b], None,
                                    ALU.is_equal).then_inc(oh_done, 1)
                rolled(dve, NPP, [(one_hots, 0)])
                dve.wait_ge(oh_used, NPP)
                v.tensor_copy(starts[:, :], ps_mask[:, 0:T]).then_inc(hist_read, 1)
                dve.wait_ge(hist_read, 1)
                v.tensor_scalar(goes_on[:, :], starts[:, :], -1.0, 1.0, ALU.mult, ALU.add)
                dve.wait_ge(prefix_done, 1)
                link(dve, v.tensor_copy(total[:, :], ps_r[:, 256:256 + T]))
                link(dve, v.tensor_tensor_scan(out=upto[:, :], data0=total[:, :], data1=zeros[:, :], initial=-1.0,
                                               op0=ALU.add, op1=ALU.add))
                link(dve, v.tensor_tensor(upto[:, :], upto[:, :], total[:, :], ALU.subtract))
                link(dve, v.tensor_tensor(s_node[:, :], upto[:, :], ps_r[:, 0:T], ALU.add))
                v.tensor_copy(s_index[:, :, 1], s_node[:, :])
                link(dve, v.tensor_tensor(s_chunk[:, :], slotf[:, :], s_node[:, :], ALU.subtract))
                v.tensor_scalar(s_index[:, :, 0], s_chunk[:, :], float(CHUNKS - 1), None, ALU.min)
                for l in range(L):
                    v.tensor_scalar(s_edge[:, :, l], s_chunk[:, :], float(L), float(l), ALU.mult, ALU.add)

        ea_in = [sem(f"ea_in{k}") for k in range(2)]
        ug_in = [sem(f"ug_in{k}") for k in range(2)]
        rows_out = [sem(f"rows_out{k}") for k in range(2)]
        idx_done = sem("idx_done")
        turned = sem("turned")
        eaT_done = sem("eaT_done")
        past_done = sem("past_done")
        inv_done = sem("inv_done")
        z_done = sem("z_done")
        rp_done = sem("rp_done")
        half_done = sem("half_done")
        rsum_done = sem("rsum_done")
        m_done = sem("m_done")
        mask_done = sem("mask_done")
        mred_done = sem("mred_done")
        scan_done = sem("scan_done")
        r_turned = sem("r_turned")
        rT_done = sem("rT_done")

        with nc.Block() as block:
            @block.gpsimd
            def _(pool):
                def take_index(i, k):
                    t = 2 * i + k
                    if not (isinstance(i, int) and i == 0):
                        pool.wait_ge(ea_in[k], 16 * i)
                        pool.wait_ge(ug_in[k], 16 * i)
                    nc.gpsimd.tensor_copy(idx[:, k, :], s_index[:, bass.ds(t, 1), :]).then_inc(idx_done, 1)

                def gather(i, k):
                    t = 2 * i + k
                    at_least(pool, idx_done, t + 1)
                    at_least(pool, turned, t - 1)
                    at_least(pool, inv_done, t - 1, alone=True)
                    pool.indirect_dma_start(
                        out=ea[:, k, :], out_offset=None, in_=chunk_rows,
                        in_offset=bass.IndirectOffsetOnAxis(ap=idx[:, k, 0:1], axis=0)
                    ).then_inc(ea_in[k], 16)
                    pool.indirect_dma_start(
                        out=ug[:, k, :], out_offset=None, in_=utab,
                        in_offset=bass.IndirectOffsetOnAxis(ap=idx[:, k, 1:2], axis=0)
                    ).then_inc(ug_in[k], 16)

                def sum_edges(i, k):
                    t = 2 * i + k
                    at_least(pool, rp_done, t + 1)
                    nc.gpsimd.tensor_tensor(half[:, k, :, :], rp[:, k, 0:2, :], rp[:, k, 2:4, :],
                                            ALU.add).then_inc(half_done, 1)
                    at_least(pool, half_done, t + 1)
                    at_least(pool, scan_done, t - 1)
                    nc.gpsimd.tensor_tensor(rsum[:, k, :], half[:, k, 0, :], half[:, k, 1, :],
                                            ALU.add).then_inc(rsum_done, 1)
                rolled(pool, T, [(take_index, 3), (sum_edges, 0), (gather, 3)])

            @block.tensor
            def _(pe):
                def turn(i, k):
                    t = 2 * i + k
                    pe.wait_ge(ea_in[k], 16 * i + 16)
                    pe.wait_ge(ug_in[k], 16 * i + 16)
                    at_least(pe, eaT_done, t - 1)
                    nc.tensor.transpose(ps_t[k][:, 0:P], ea[:, k, 0:P], ident[:, :])
                    nc.tensor.transpose(ps_t[k][:, P:2 * P], ea[:, k, P:2 * P], ident[:, :])
                    nc.tensor.transpose(ps_t[k][:, 2 * P:3 * P], ug[:, k, 0:F], ident[:, :]).then_inc(turned, 1)

                def drop_others(k, out):
                    for l in range(L):
                        last = nc.tensor.matmul(out[:, l * P:(l + 1) * P], inv[:, k, l:l + 1].broadcast_to([P, P]),
                                                neg_ident[:, :], start=False, stop=l == L - 1,
                                                skip_group_check=True)
                    return last

                def edge_product(i, k):
                    t = 2 * i + k
                    at_least(pe, eaT_done, t + 1)
                    at_least(pe, inv_done, t + 1)
                    z = ps_z[k].rearrange("f (j r s) -> f j r s", j=L // 2, r=2)
                    for r in range(2):
                        nc.tensor.matmul(z[:, :, r, :], w1b[:, r, :], eaT[:, k, :, :], start=r == 0, stop=False,
                                         skip_group_check=True)
                    drop_others(k, ps_z[k]).then_inc(z_done, 1)

                def message(i, k):
                    t = 2 * i + k
                    at_least(pe, rp_done, t + 1)
                    at_least(pe, scan_done, t - 1)
                    nc.tensor.matmul(ps_m[k][:, :], w2[:, :], rp[:, k, :, :], start=True, stop=False,
                                     skip_group_check=True)
                    drop_others(k, ps_m[k]).then_inc(m_done, 1)
                    at_least(pe, scan_done, t)
                    nc.tensor.matmul(ps_mask[:, 0:P], starts[:, bass.ds(t, 1)].broadcast_to([P, P]),
                                     neg_ident[:, :], start=True, stop=True)
                    nc.tensor.matmul(ps_mask[:, P:2 * P], goes_on[:, bass.ds(t, 1)].broadcast_to([P, P]),
                                     identb[:, :], start=True, stop=True).then_inc(mask_done, 1)

                def turn_scans(i, k):
                    t = 2 * i + k
                    at_least(pe, scan_done, t + 1)
                    at_least(pe, rT_done, t)
                    nc.tensor.transpose(ps_r[:, 0:P], smax[:, k, :], ident[:, :])
                    nc.tensor.transpose(ps_r[:, P:2 * P], ssum[:, k, :], ident[:, :]).then_inc(r_turned, 1)
                rolled(pe, T, [(turn, 1), (edge_product, 0), (message, -1), (turn_scans, -2)])

            @block.scalar
            def _(act):
                def take_turned(i, k):
                    t = 2 * i + k
                    at_least(act, turned, t + 1)
                    at_least(act, rp_done, t - 1)
                    nc.scalar.activation(eaT[:, k, :, :], ps_t[k][:, 0:2 * P], ACT.Copy)
                    nc.scalar.activation(nuT[:, k, :], ps_t[k][:, 2 * P:3 * P], ACT.Copy,
                                         scale=-1.0).then_inc(eaT_done, 1)

                def take_rows(i, k):
                    t = 2 * i + k
                    at_least(act, r_turned, t + 1)
                    at_least(act, rows_out[k], 16 * i)
                    nc.scalar.activation(rT[:, k, :], ps_r[:, 0:2 * P], ACT.Copy).then_inc(rT_done, 1)
                rolled(act, T, [(take_turned, 1), (take_rows, -2)])

            @block.sync
            def _(sp):
                def store(i, k):
                    t = 2 * i + k
                    at_least(sp, rT_done, t + 1)
                    sp.dma_start(rtab[bass.ds(t * P, P), :], rT[:, k, :]).then_inc(rows_out[k], 16)
                rolled(sp, T, [(store, 0)])
                sp.wait_ge(rows_out[0], 16 * ((T + 1) // 2))
                sp.wait_ge(rows_out[1], 16 * (T // 2))

            @block.vector
            def _(dve):
                v = nc.vector

                def find_past(i, k):
                    t = 2 * i + k
                    dve.wait_ge(ug_in[k], 16 * i + 16)
                    v.tensor_scalar(past[:, k, :], s_edge[:, bass.ds(t, 1), :], ug[:, k, F + 1:F + 2], None,
                                    ALU.is_ge).then_inc(past_done, 1)

                def find_inv(i, k):
                    t = 2 * i + k
                    at_least(dve, past_done, t + 1)
                    at_least(dve, m_done, t - 1)
                    v.scalar_tensor_tensor(inv[:, k, :], s_edge[:, bass.ds(t, 1), :], ug[:, k, F:F + 1],
                                           past[:, k, :], ALU.is_lt, ALU.add).then_inc(inv_done, 1)

                def relu_less_u(i, k):
                    t = 2 * i + k
                    at_least(dve, z_done, t + 1)
                    at_least(dve, m_done, t - 1)
                    at_least(dve, rsum_done, t - 1)
                    v.tensor_tensor(rp[:, k, :, :], ps_z[k].rearrange("f (l s) -> f l s", l=L),
                                    nuT[:, k:k + 1, :].broadcast_to([P, L, P]), ALU.max).then_inc(rp_done, 1)

                def reduce_message(i, k):
                    t = 2 * i + k
                    at_least(dve, m_done, t + 1)
                    v.tensor_reduce(mred[:, k, :], ps_m[k].rearrange("f (l s) -> f s l", l=L), AX.X,
                                    ALU.max).then_inc(mred_done, 1)

                def scan(i, k):
                    t = 2 * i + k
                    at_least(dve, rsum_done, t + 1)
                    at_least(dve, mask_done, t + 1)
                    at_least(dve, mred_done, t + 1)
                    at_least(dve, scan_done, t)
                    at_least(dve, r_turned, t - 1)
                    first = isinstance(t, int) and t == 0
                    v.tensor_tensor_scan(out=ssum[:, k, :], data0=ps_mask[:, P:2 * P], data1=rsum[:, k, :],
                                         initial=0.0 if first else ssum[:, 1 - k, P - 1:P], op0=ALU.mult,
                                         op1=ALU.add)
                    v.tensor_tensor_scan(out=smax[:, k, :], data0=ps_mask[:, 0:P], data1=mred[:, k, :],
                                         initial=-BIG if first else smax[:, 1 - k, P - 1:P], op0=ALU.add,
                                         op1=ALU.max).then_inc(scan_done, 1)
                rolled(dve, T, [(find_past, 1), (reduce_message, -1), (find_inv, 1), (relu_less_u, 0), (scan, -1)])

        rg_in = [sem(f"rg_in{k}") for k in range(2)]
        ridx_done = sem("ridx_done")
        bias_done = sem("bias_done")
        su_done = sem("su_done")
        uc_done = sem("uc_done")
        su_turned = sem("su_turned")
        suT_done = sem("suT_done")
        sw_done = sem("sw_done")
        am_done = sem("am_done")
        ag_done = sem("ag_done")
        ag_turned = sem("ag_turned")
        agT_done = sem("agT_done")
        o_done = sem("o_done")
        o_mid = sem("o_mid")
        o_ready = sem("o_ready")
        out_out = sem("out_out")
        ps_s, ps_g, ps_a, ps_o = bank[0:2], bank[2:4], bank[4:6], bank[6:8]

        with nc.Block() as block:
            @block.gpsimd
            def _(pool):
                def gather(i, k):
                    b = 2 * i + k
                    if not (isinstance(i, int) and i == 0):
                        pool.wait_ge(rg_in[k], 16 * i)
                    nc.gpsimd.tensor_copy(ridx[:, k, :], gendi[:, bass.ds(b, 1)]).then_inc(ridx_done, 1)
                    at_least(pool, ridx_done, b + 1)
                    at_least(pool, ag_done, b - 1, alone=True)
                    pool.indirect_dma_start(
                        out=rg[:, k, :], out_offset=None, in_=rtab,
                        in_offset=bass.IndirectOffsetOnAxis(ap=ridx[:, k, :], axis=0)
                    ).then_inc(rg_in[k], 16)
                rolled(pool, NPP, [(gather, 0)])

            @block.scalar
            def _(act):
                def copy_u(i, k):
                    b = 2 * i + k
                    at_least(act, su_turned, b - 1)
                    nc.scalar.activation(su[:, k, 1, :], us[:, bass.ds(b, 1), 0:F], ACT.Copy).then_inc(uc_done, 1)

                def take_su(i, k):
                    b = 2 * i + k
                    at_least(act, su_turned, b + 1)
                    at_least(act, sw_done, b - 1)
                    nc.scalar.activation(suT[:, k, :, :], ps_s[k][:, 0:2 * P], ACT.Copy).then_inc(suT_done, 1)

                def take_ag(i, k):
                    b = 2 * i + k
                    at_least(act, ag_turned, b + 1)
                    at_least(act, o_done, b - 1)
                    nc.scalar.activation(agT[:, k, :, :], ps_a[k][:, 0:2 * P], ACT.Copy).then_inc(agT_done, 1)
                rolled(act, NPP, [(copy_u, 1), (take_su, 0), (take_ag, -1)])

            @block.tensor
            def _(pe):
                def turn_su(i, k):
                    b = 2 * i + k
                    at_least(pe, su_done, b + 1)
                    at_least(pe, uc_done, b + 1)
                    at_least(pe, suT_done, b - 1)
                    nc.tensor.transpose(ps_s[k][:, 0:P], su[:, k, 0, :], ident[:, :])
                    nc.tensor.transpose(ps_s[k][:, P:2 * P], su[:, k, 1, :], ident[:, :]).then_inc(su_turned, 1)

                def by_w2(i, k):
                    b = 2 * i + k
                    at_least(pe, suT_done, b + 1)
                    at_least(pe, ag_done, b - 1)
                    for j in range(2):
                        last = nc.tensor.matmul(ps_g[k][:, j * F:(j + 1) * F], suT[:, k, j, :], w2[:, :], start=True,
                                                stop=True)
                    last.then_inc(sw_done, 1)

                def turn_ag(i, k):
                    b = 2 * i + k
                    at_least(pe, ag_done, b + 1)
                    at_least(pe, agT_done, b - 1)
                    nc.tensor.transpose(ps_a[k][:, 0:P], ag[:, k, 0, :], ident[:, :])
                    nc.tensor.transpose(ps_a[k][:, P:2 * P], ag[:, k, 1, :], ident[:, :]).then_inc(ag_turned, 1)

                def outputs(i, k):
                    b = 2 * i + k
                    at_least(pe, agT_done, b + 1)
                    at_least(pe, o_ready, b - 1)
                    nc.tensor.matmul(ps_o[k][:, 0:F], agT[:, k, 0, :], ws[:, :], start=True, stop=False)
                    nc.tensor.matmul(ps_o[k][:, 0:F], agT[:, k, 1, :], wx[:, :], start=False, stop=True)
                    nc.tensor.matmul(ps_o[k][:, F:2 * F], agT[:, k, 0, :], wm[:, :], start=True,
                                     stop=True).then_inc(o_done, 1)
                rolled(pe, NPP, [(turn_su, 1), (by_w2, 0), (turn_ag, -1), (outputs, -1)])

            @block.vector
            def _(dve):
                v = nc.vector
                v.tensor_tensor(bor[:, 0, :], bor[:, 0, :], bor[:, 1, :], ALU.add).then_inc(bias_done, 1)
                dve.wait_ge(bias_done, 1)
                v.tensor_tensor(bor[:, 0, :], bor[:, 0, :], bor[:, 2, :], ALU.add).then_inc(bias_done, 1)
                dve.wait_ge(bias_done, 2)
                v.tensor_tensor(xs[:, :, :], xs[:, :, :], bor[:, 0:1, :].broadcast_to([P, NPP, F]),
                                ALU.add).then_inc(bias_done, 1)
                dve.wait_ge(bias_done, 3)

                def sum_relu(i, k):
                    b = 2 * i + k
                    dve.wait_ge(rg_in[k], 16 * i + 16)
                    at_least(dve, su_turned, b - 1)
                    v.scalar_tensor_tensor(su[:, k, 0, :], us[:, bass.ds(b, 1), 0:F], slots_l[:, bass.ds(b, 1)],
                                           rg[:, k, F:2 * F], ALU.mult, ALU.add).then_inc(su_done, 1)

                def with_bias(i, k):
                    b = 2 * i + k
                    at_least(dve, ag_turned, b - 1)
                    v.tensor_tensor(am[:, k, 0, :], rg[:, k, 0:F], b2r[:, :], ALU.add).then_inc(am_done, 1)
                    at_least(dve, sw_done, b + 1)
                    v.scalar_tensor_tensor(ag[:, k, 0, :], b2r[:, :], count[:, bass.ds(b, 1)], ps_g[k][:, 0:F],
                                           ALU.mult, ALU.add)
                    at_least(dve, am_done, 2 * b + 1)
                    v.tensor_tensor(am[:, k, 1, :], am[:, k, 0, :], ps_g[k][:, F:2 * F], ALU.add).then_inc(am_done, 1)
                    at_least(dve, am_done, 2 * b + 2)
                    v.tensor_scalar(ag[:, k, 1, :], am[:, k, 1, :], some[:, bass.ds(b, 1)], None,
                                    ALU.mult).then_inc(ag_done, 1)

                def finish(i, k):
                    b = 2 * i + k
                    at_least(dve, o_done, b + 1)
                    v.scalar_tensor_tensor(ob[:, k, :], ps_o[k][:, F:2 * F], rcount[:, bass.ds(b, 1)],
                                           xs[:, bass.ds(b, 1), :], ALU.mult, ALU.add).then_inc(o_mid, 1)
                    at_least(dve, o_mid, b + 1)
                    v.tensor_tensor(xs[:, bass.ds(b, 1), :], ob[:, k, :], ps_o[k][:, 0:F],
                                    ALU.add).then_inc(o_ready, 1)
                rolled(dve, NPP, [(sum_relu, 1), (with_bias, 0), (finish, -1)])

            @block.sync
            def _(sp):
                sp.wait_ge(o_ready, NPP)
                for p0, p1, nb, rows in node_rows(out):
                    sp.dma_start(rows, xs[p0:p1, 0:nb, :]).then_inc(out_out, 16)
                sp.wait_ge(out_out, 16 * 3)


_INS = ["x", "dst", "edge_attr_64", "L0_gnn_W1", "L0_gnn_b1", "L0_gnn_W2", "L0_gnn_b2", "L0_gnn_Wm", "L0_gnn_bm",
        "L0_gnn_Wx", "L0_gnn_bx", "L0_gnn_Ws", "L0_gnn_bs"]


def kernel(**inputs):
    import numpy as np

    import concourse.bacc as bacc
    from concourse.bass_utils import run_bass_kernel_spmd

    nc = bacc.Bacc("TRN2", target_bir_lowering=False, num_devices=1)
    arrays, args = {}, []
    for name in _INS:
        a = np.ascontiguousarray(inputs[name])
        arrays[f"in_{name}"] = a
        args.append(nc.dram_tensor(f"in_{name}", a.shape, mybir.dt.from_np(a.dtype), kind="ExternalInput").ap())
    args.append(nc.dram_tensor("out_0", inputs["x"].shape, F32, kind="ExternalOutput").ap())
    gnn_kernel(nc, *args)
    r = run_bass_kernel_spmd(nc, [arrays], core_ids=[0])
    return r.results[0]["out_0"]
```

```python
from contextlib import ExitStack

import concourse.bass as bass
from concourse import mybir

F32 = mybir.dt.float32
BF16 = mybir.dt.bfloat16
I32 = mybir.dt.int32
ALU = mybir.AluOpType
ACT = mybir.ActivationFunctionType
AX = mybir.AxisListType

P = 128
BIG = 1e30
EPS = 1e-5


def at_least(engine, semaphore, value, alone=False):
    if isinstance(value, int) and value <= 0:
        return
    engine.wait_ge(semaphore, value)
    if alone:
        engine.nop(nofuse=True)


U = 4


def rolled(engine, n, order):
    least, most = min(o for _, o in order), max(o for _, o in order)
    first = -(least // U) * U + U
    last = n - most
    last -= (last - first) % U

    def at(t):
        for step, o in order:
            if 0 <= t + o < n:
                step((t + o) // U, (t + o) % U)
    for t in range(-most, first):
        at(t)
    with engine.Fori(first // U, last // U) as i:
        for k in range(U):
            for step, o in order:
                step(i + (k + o) // U, (k + o) % U)
    for t in range(last, n - least):
        at(t)


def gnn_kernel(nc, x, dst, edge, W1, b1, W2, b2, Wm, bm, Wx, bx, Ws, bs, out):
    N, F = x.shape
    E, FE = edge.shape
    assert F == P and 2 * FE == P
    L = 4
    NPP = -(-N // P)
    FULL = N // NPP
    REST = N - FULL * NPP
    EVEN = FULL // 16 * 16
    CHUNKS = E // L
    T = -(-(CHUNKS + NPP * P) // P)
    BS = 250
    NB = E // BS
    assert FULL == P - 1 and E % BS == 0 and E % L == 0 and T < 256 and T % 2

    utab = nc.dram_tensor("utab", (NPP * P, F), F32, kind="Internal").ap()
    rtab = nc.dram_tensor("rtab", (T * P, 2 * F), F32, kind="Internal").ap()
    chunk_rows = edge.rearrange("(c l) f -> c (l f)", l=L)
    search_rows = dst.rearrange("(a b) -> a b", b=BS)

    def node_rows(a):
        whole = a[0:FULL * NPP, :].rearrange("(p b) f -> p b f", b=NPP)
        return ((0, EVEN, NPP, whole[0:EVEN]), (EVEN, FULL, NPP, whole[EVEN:FULL]),
                (FULL, FULL + 1, REST, a[FULL * NPP:N, :].rearrange("(p b) f -> p b f", b=REST)))

    with ExitStack() as ctx:
        def sb(name, shape, dt=F32):
            return ctx.enter_context(nc.sbuf_tensor(name, shape, dt))

        def sem(name):
            return ctx.enter_context(nc.semaphore(name))

        bank = [ctx.enter_context(nc.psum_tensor(f"bank{i}", [P, 512], F32)) for i in range(8)]
        ps_z, ps_m, ps_t, ps_mask, ps_r = bank[0:2], bank[2:4], bank[4:6], bank[6], bank[7]

        ident = sb("ident", [P, P])
        identb = sb("identb", [P, P], BF16)
        neg_ident = sb("neg_ident", [P, P], BF16)
        onesb = sb("onesb", [P, P], BF16)
        ones = sb("ones", [P, P])
        trif = sb("trif", [P, P])
        tri = sb("tri", [P, P], BF16)
        iota_i = sb("iota_i", [P, 256], I32)
        iotab = sb("iotab", [P, 256], BF16)
        w1a = sb("w1a", [P, F])
        w1b = sb("w1b", [P, 2, F])
        w2 = sb("w2", [P, F])
        wm = sb("wm", [P, F])
        wx = sb("wx", [P, F])
        ws = sb("ws", [P, F])
        b1r = sb("b1r", [P, F])
        b2r = sb("b2r", [P, F])
        bor = sb("bor", [P, 3, F])
        xs = sb("xs", [P, NPP, F])
        us = sb("us", [P, NPP, F])
        nodei = sb("nodei", [P, NPP + 1], I32)
        nodef = sb("nodef", [P, NPP + 1])
        stats = sb("stats", [P, NPP, 6])
        mv = sb("mv", [P, NPP, 2])
        sd = sb("sd", [P, 4, NPP])
        rstd = sb("rstd", [P, NPP])
        coarse = sb("coarse", [P, NPP + 1])
        coarsei = sb("coarsei", [P, NPP + 1], I32)
        fine = sb("fine", [P, NPP + 1])
        start = sb("start", [P, NPP + 1])
        count = sb("count", [P, NPP])
        rcount = sb("rcount", [P, NPP])
        some = sb("some", [P, NPP])
        wi = sb("wi", [P, 4, NPP], I32)
        wf = sb("wf", [P, 4, NPP])
        goff = sb("goff", [P, NPP])
        gend = sb("gend", [P, NPP])
        gendi = sb("gendi", [P, NPP], I32)
        slots_l = sb("slots_l", [P, NPP])
        slotf = sb("slotf", [P, T])
        sloti = sb("sloti", [P, T], I32)
        starts = sb("starts", [P, T], BF16)
        goes_on = sb("goes_on", [P, T], BF16)
        total = sb("total", [P, T])
        zeros = sb("zeros", [P, T])
        upto = sb("upto", [P, T])
        s_node = sb("s_node", [P, T])
        s_chunk = sb("s_chunk", [P, T])
        s_index = sb("s_index", [P, T], I32)
        s_first = sb("s_first", [P, T])
        s_end = sb("s_end", [P, T])
        hist = sb("hist", [P, T])
        s_edge = sb("s_edge", [P, T, L])
        late = sb("late", [P, T, L])
        inv = sb("inv", [P, T, L], BF16)
        base = sb("base", [1, T])
        base_i = sb("base_i", [1, T], I32)
        s_rel = sb("s_rel", [P, T], BF16)
        row = sb("row", [P, 1])
        row_i = sb("row_i", [P, 1], I32)
        stage = ctx.enter_context(ExitStack())

        def ring(name, shape, dt=F32):
            return stage.enter_context(nc.sbuf_tensor(name, shape, dt))

        last_i = ring("last_i", [1, NB], I32)
        last_f = ring("last_f", [1, NB])
        lasts = ring("lasts", [P, NB])
        found = ring("found", [P, NPP + 1, BS], I32)
        junk = ring("junk", [P, U, NB])
        oh_lo = ring("oh_lo", [P, U, P])
        oh_hi = ring("oh_hi", [P, U, T])
        oh_c = ring("oh_c", [P, U, 2, T])
        hn = ring("hn", [P, U, F])
        hT = ring("hT", [P, U, F])
        x_in = sem("x_in")
        w_in = sem("w_in")
        last_in = sem("last_in")
        const_done = sem("const_done")
        pool_chain = sem("pool_chain")
        dve_chain = sem("dve_chain")
        lasts_bc = sem("lasts_bc")
        coarse_done = sem("coarse_done")
        coarse_step = sem("coarse_step")
        fine_step = sem("fine_step")
        stats_done = sem("stats_done")
        lasts_ready = sem("lasts_ready")
        found_in = sem("found_in")
        var_done = sem("var_done")
        sd_done = sem("sd_done")
        h_done = sem("h_done")
        h_turned = sem("h_turned")
        hT_done = sem("hT_done")
        u_done = sem("u_done")
        u_read = sem("u_read")
        oh_done = sem("oh_done")
        oh_used = sem("oh_used")
        hist_read = sem("hist_read")
        prefix_done = sem("prefix_done")
        base_done = sem("base_done")
        base_bc = sem("base_bc")
        utab_out = sem("utab_out")
        chain = [0]

        def link(dve, instruction):
            chain[0] += 1
            instruction.then_inc(dve_chain, 1)
            dve.wait_ge(dve_chain, chain[0])

        X_DMAS = 3
        with nc.Block() as block:
            @block.sync
            def _(sp):
                sp.dma_start(last_i[:, :], search_rows[:, BS - 1:BS].rearrange("a b -> b a"),
                             allow_slow_non_contiguous=True).then_inc(last_in, 16)
                sp.wait_ge(const_done, 1)
                for p0, p1, nb, rows in node_rows(x):
                    sp.dma_start(xs[p0:p1, 0:nb, :], rows).then_inc(x_in, 16)
                sp.wait_ge(u_read, NPP)
                sp.dma_start(utab.rearrange("(p b) f -> p b f", b=NPP), us[:, :, :]).then_inc(utab_out, 16)
                sp.wait_ge(utab_out, 16)

            @block.scalar
            def _(act):
                act.dma_start(w1a[:, :], W1[0:F, :]).then_inc(w_in, 16)
                act.wait_ge(const_done, 1)
                act.dma_start(w1b[0:FE, 0, :], W1[F:F + FE, :]).then_inc(w_in, 16)
                act.dma_start(w1b[FE:P, 1, :], W1[F:F + FE, :]).then_inc(w_in, 16)
                for t, a in ((w2, W2), (wm, Wm), (wx, Wx), (ws, Ws)):
                    act.dma_start(t[:, :], a).then_inc(w_in, 16)
                for t, a in ((b1r[:, :], b1), (b2r[:, :], b2), (bor[:, 0, :], bm), (bor[:, 1, :], bx),
                             (bor[:, 2, :], bs)):
                    act.dma_start(t, a.rearrange("(a f) -> a f", a=1).broadcast_to([P, F])).then_inc(w_in, 16)
                act.wait_ge(var_done, 1)
                nc.scalar.activation(sd[:, 0, :], sd[:, 1, :], ACT.Sqrt).then_inc(sd_done, 1)

                def relu_h(i, k):
                    at_least(act, h_turned, U * i + k + 1)
                    at_least(act, u_done, U * i + k - 1)
                    nc.scalar.activation(hT[:, k, :], ps_t[k % 2][:, 0:F], ACT.Relu).then_inc(hT_done, 1)
                rolled(act, NPP, [(relu_h, 0)])

            @block.gpsimd
            def _(pool):
                nc.gpsimd.memset(xs[:, REST:NPP, :], 0.0)
                nc.gpsimd.memset(w1b[:, :, :], 0.0).then_inc(const_done, 1)
                nc.gpsimd.iota(nodei[:, :], pattern=[[1, NPP + 1]], base=0, channel_multiplier=NPP)
                nc.gpsimd.iota(iota_i[:, :], pattern=[[1, 256]], base=0, channel_multiplier=0)
                nc.gpsimd.iota(sloti[:, :], pattern=[[P, T]], base=0, channel_multiplier=1)
                nc.gpsimd.memset(ident[:, :], 0.0)
                nc.gpsimd.memset(identb[:, :], 0.0)
                nc.gpsimd.memset(neg_ident[:, :], 0.0)
                nc.gpsimd.memset(onesb[:, :], 1.0)
                nc.gpsimd.memset(ones[:, :], 1.0)
                nc.gpsimd.iota(row_i[:, :], pattern=[[1, 1]], base=0, channel_multiplier=1)
                nc.gpsimd.memset(zeros[:, :], 0.0)
                nc.gpsimd.memset(tri[:, :], 1.0).then_inc(pool_chain, 1)
                pool.wait_ge(pool_chain, 1)
                for m, v in ((ident, 1.0), (identb, 1.0), (neg_ident, -BIG)):
                    nc.gpsimd.affine_select(out=m[:, :], in_=m[:, :], compare_op=ALU.not_equal, fill=v, base=0,
                                            pattern=[[-1, P]], channel_multiplier=1)
                nc.gpsimd.affine_select(out=tri[:, :], in_=tri[:, :], compare_op=ALU.is_ge, fill=0.0, base=0,
                                        pattern=[[1, P]], channel_multiplier=-1).then_inc(const_done, 1)
                nc.gpsimd.affine_select(out=trif[:, :], in_=ones[:, :], compare_op=ALU.is_ge, fill=0.0, base=0,
                                        pattern=[[1, P]], channel_multiplier=-1).then_inc(const_done, 1)
                pool.wait_ge(coarse_done, 1)
                for b in range(NPP + 1):
                    pool.indirect_dma_start(
                        out=found[:, b, :], out_offset=None, in_=search_rows,
                        in_offset=bass.IndirectOffsetOnAxis(ap=coarsei[:, b:b + 1], axis=0)).then_inc(found_in, 16)

            @block.tensor
            def _(pe):
                pe.wait_ge(const_done, 3)
                pe.wait_ge(lasts_ready, 1)
                nc.tensor.matmul(ps_z[0][:, 0:NB], ones[0:1, :], last_f[0:1, :], start=True,
                                 stop=True).then_inc(lasts_bc, 1)
                pe.wait_ge(w_in, 16 * 12)

                def u_product(i, k):
                    at_least(pe, h_done, U * i + k + 1)
                    nc.tensor.transpose(ps_t[k % 2][:, 0:F], hn[:, k, :], ident[:, :]).then_inc(h_turned, 1)
                    at_least(pe, hT_done, U * i + k + 1)
                    at_least(pe, u_read, U * i + k - 1)
                    nc.tensor.matmul(ps_m[k % 2][:, 0:F], hT[:, k, :], w1a[:, :], start=True,
                                     stop=True).then_inc(u_done, 1)
                rolled(pe, NPP, [(u_product, 0)])

                def add_nodes(i, k):
                    b = U * i + k
                    at_least(pe, oh_done, b + 1)
                    is_int = isinstance(b, int)
                    for bank_, hot in ((ps_mask, oh_hi[:, k, :]), (ps_z[0], oh_c[:, k, 0, :]),
                                       (ps_z[1], oh_c[:, k, 1, :])):
                        last = nc.tensor.matmul(bank_[:, 0:T], oh_lo[:, k, :], hot, start=is_int and b == 0,
                                                stop=is_int and b == NPP - 1)
                    last.then_inc(oh_used, 1)
                rolled(pe, NPP, [(add_nodes, 0)])
                pe.wait_ge(hist_read, 1)
                nc.tensor.matmul(ps_r[:, 0:T], tri[:, :], starts[:, :], start=True, stop=True)
                nc.tensor.matmul(ps_r[:, 256:256 + T], onesb[:, :], starts[:, :], start=True, stop=True)
                nc.tensor.matmul(ps_m[0][:, 0:T], trif[:, :], hist[:, :], start=True, stop=True)
                nc.tensor.matmul(ps_m[0][:, 256:256 + T], ones[:, :], hist[:, :], start=True,
                                 stop=True).then_inc(prefix_done, 1)
                pe.wait_ge(base_done, 1)
                nc.tensor.matmul(ps_z[0][:, 0:T], ones[0:1, :], base[0:1, :], start=True, stop=True).then_inc(base_bc, 1)

            @block.vector
            def _(dve):
                v = nc.vector
                dve.wait_ge(const_done, 3)
                v.tensor_copy(iotab[:, :], iota_i[:, :])
                v.tensor_copy(nodef[:, :], nodei[:, :])
                v.tensor_copy(slotf[:, :], sloti[:, :])
                dve.wait_ge(last_in, 16)
                v.tensor_copy(last_f[:, :], last_i[:, :]).then_inc(lasts_ready, 1)
                dve.wait_ge(lasts_bc, 1)
                link(dve, v.tensor_copy(lasts[:, :], ps_z[0][:, 0:NB]))
                def count_blocks(i, k):
                    b = U * i + k
                    at_least(dve, coarse_step, b - 1)
                    v.tensor_scalar(junk[:, k, :], lasts[:, :], nodef[:, bass.ds(b, 1)], 0.0, ALU.is_lt, ALU.add,
                                    accum_out=coarse[:, bass.ds(b, 1)]).then_inc(coarse_step, 1)
                rolled(dve, NPP + 1, [(count_blocks, 0)])
                dve.wait_ge(coarse_step, NPP + 1)
                v.tensor_copy(row[:, :], row_i[:, :])
                link(dve, v.tensor_scalar(coarse[:, :], coarse[:, :], float(NB - 1), None, ALU.min))
                v.tensor_copy(coarsei[:, :], coarse[:, :]).then_inc(coarse_done, 1)

                dve.wait_ge(x_in, 16 * X_DMAS)
                def row_stats(i, k):
                    b = bass.ds(U * i + k, 1)
                    v.bn_stats(stats[:, b, :], xs[:, b, :]).then_inc(stats_done, 1)
                rolled(dve, NPP, [(row_stats, 0)])
                dve.wait_ge(stats_done, NPP)
                for b in range(NPP):
                    last = v.bn_aggr(mv[:, b, :], stats[:, b, :])
                link(dve, last)
                v.tensor_scalar(sd[:, 1, :], mv[:, :, 1], EPS, None, ALU.add).then_inc(var_done, 1)
                dve.wait_ge(sd_done, 1)
                link(dve, v.reciprocal(sd[:, 2, :], sd[:, 0, :]))
                link(dve, v.tensor_tensor(sd[:, 3, :], sd[:, 1, :], sd[:, 2, :], ALU.mult))
                link(dve, v.tensor_tensor(sd[:, 2, :], sd[:, 3, :], sd[:, 0, :], ALU.add))
                link(dve, v.tensor_scalar(sd[:, 3, :], sd[:, 2, :], 0.5, None, ALU.mult))
                link(dve, v.reciprocal(rstd[:, :], sd[:, 3, :]))
                dve.wait_ge(w_in, 16 * 12)

                def normalise(i, k):
                    b = U * i + k
                    at_least(dve, h_turned, b - 1)
                    v.tensor_scalar(hn[:, k, :], xs[:, bass.ds(b, 1), :], mv[:, bass.ds(b, 1), 0],
                                    rstd[:, bass.ds(b, 1)], ALU.subtract, ALU.mult).then_inc(h_done, 1)

                def add_b1(i, k):
                    at_least(dve, u_done, U * i + k + 1)
                    v.tensor_tensor(us[:, bass.ds(U * i + k, 1), :], ps_m[k % 2][:, 0:F], b1r[:, :],
                                    ALU.add).then_inc(u_read, 1)

                rolled(dve, NPP, [(normalise, 0), (add_b1, -1)])

                dve.wait_ge(found_in, 16 * (NPP + 1))
                def count_edges(i, k):
                    b = U * i + k
                    at_least(dve, fine_step, b - 1)
                    v.tensor_scalar(junk[:, k, 0:BS], found[:, bass.ds(b, 1), :], nodef[:, bass.ds(b, 1)], 0.0,
                                    ALU.is_lt, ALU.add, accum_out=fine[:, bass.ds(b, 1)]).then_inc(fine_step, 1)
                rolled(dve, NPP + 1, [(count_edges, 0)])
                dve.wait_ge(fine_step, NPP + 1)
                link(dve, v.scalar_tensor_tensor(start[:, :], coarse[:, :], float(BS), fine[:, :], ALU.mult,
                                                 ALU.add))
                first, end = start[:, 0:NPP], start[:, 1:NPP + 1]
                v.tensor_copy(wi[:, 0, :], first)
                v.scalar_tensor_tensor(wf[:, 0, :], end, -1.0, first, ALU.add, ALU.max)
                link(dve, v.tensor_tensor(count[:, :], end, first, ALU.subtract))
                v.tensor_copy(wi[:, 1, :], wf[:, 0, :])
                v.tensor_scalar(wf[:, 1, :], count[:, :], 1.0, None, ALU.max)
                link(dve, v.tensor_scalar(some[:, :], count[:, :], 0.0, None, ALU.is_gt))
                v.reciprocal(rcount[:, :], wf[:, 1, :])
                shift = (L - 1).bit_length()
                link(dve, v.tensor_scalar(wi[:, 2:4, :], wi[:, 0:2, :], shift, None, ALU.logical_shift_right))
                link(dve, v.tensor_copy(wf[:, 2:4, :], wi[:, 2:4, :]))
                v.tensor_tensor(goff[:, :], wf[:, 2, :], nodef[:, 0:NPP], ALU.add)
                link(dve, v.tensor_tensor(gend[:, :], wf[:, 3, :], nodef[:, 0:NPP], ALU.add))
                v.tensor_copy(gendi[:, :], gend[:, :])
                v.tensor_copy(wi[:, 0, :], goff[:, :])
                link(dve, v.tensor_tensor(slots_l[:, :], gend[:, :], goff[:, :], ALU.subtract))
                v.tensor_scalar(slots_l[:, :], slots_l[:, :], 1.0, float(L), ALU.add, ALU.mult)
                v.tensor_scalar(wi[:, 1, :], wi[:, 0, :], 7, None, ALU.logical_shift_right)
                link(dve, v.tensor_scalar(wi[:, 2, :], wi[:, 0, :], P - 1, None, ALU.bitwise_and))
                link(dve, v.tensor_copy(wf[:, 1:3, :], wi[:, 1:3, :]))

                def one_hots(i, k):
                    b = bass.ds(U * i + k, 1)
                    at_least(dve, oh_used, U * i + k - 1)
                    v.tensor_scalar(oh_lo[:, k, :], iotab[:, 0:P], wf[:, 2, b], None, ALU.is_equal)
                    v.tensor_scalar(oh_hi[:, k, :], iotab[:, 0:T], wf[:, 1, b], None, ALU.is_equal)
                    v.tensor_scalar(oh_c[:, k, 0, :], iotab[:, 0:T], wf[:, 1, b], start[:, b], ALU.is_equal, ALU.mult)
                    v.tensor_scalar(oh_c[:, k, 1, :], iotab[:, 0:T], wf[:, 1, b], count[:, b], ALU.is_equal,
                                    ALU.mult).then_inc(oh_done, 1)
                rolled(dve, NPP, [(one_hots, 0)])
                dve.wait_ge(oh_used, NPP)
                v.tensor_copy(starts[:, :], ps_mask[:, 0:T])
                v.tensor_copy(s_first[:, :], ps_z[0][:, 0:T])
                v.tensor_copy(hist[:, :], ps_z[1][:, 0:T]).then_inc(hist_read, 1)
                dve.wait_ge(hist_read, 1)
                v.tensor_scalar(goes_on[:, :], starts[:, :], -1.0, 1.0, ALU.mult, ALU.add)
                dve.wait_ge(prefix_done, 1)
                for out_, sums, before in ((s_node, ps_r, -1.0), (s_end, ps_m[0], 0.0)):
                    link(dve, v.tensor_copy(total[:, :], sums[:, 256:256 + T]))
                    link(dve, v.tensor_tensor_scan(out=upto[:, :], data0=total[:, :], data1=zeros[:, :],
                                                   initial=before, op0=ALU.add, op1=ALU.add))
                    link(dve, v.tensor_tensor(upto[:, :], upto[:, :], total[:, :], ALU.subtract))
                    link(dve, v.tensor_tensor(out_[:, :], upto[:, :], sums[:, 0:T], ALU.add))
                v.tensor_scalar(base[0:1, :], s_node[0:1, :], float(NPP * P - P), None, ALU.min).then_inc(base_done, 1)
                dve.wait_ge(base_done, 1)
                v.tensor_copy(base_i[:, :], base[:, :])
                link(dve, v.tensor_tensor(s_chunk[:, :], slotf[:, :], s_node[:, :], ALU.subtract))
                v.tensor_scalar(s_index[:, :], s_chunk[:, :], float(CHUNKS - 1), None, ALU.min)
                for l in range(L):
                    last = v.tensor_scalar(s_edge[:, :, l], s_chunk[:, :], float(L), float(l), ALU.mult, ALU.add)
                link(dve, last)
                link(dve, v.tensor_tensor(late[:, :, :], s_edge[:, :, :],
                                          s_end[:, :].unsqueeze(2).broadcast_to([P, T, L]), ALU.is_ge))
                link(dve, v.tensor_tensor(s_edge[:, :, :], s_edge[:, :, :],
                                          s_first[:, :].unsqueeze(2).broadcast_to([P, T, L]), ALU.is_lt))
                v.tensor_tensor(inv[:, :, :], s_edge[:, :, :], late[:, :, :], ALU.add)
                dve.wait_ge(base_bc, 1)
                v.tensor_tensor(s_rel[:, :], s_node[:, :], ps_z[0][:, 0:T], ALU.subtract)

        stage.close()
        idx = ring("idx", [P, U, 1], I32)
        ea = ring("ea", [P, U, L * FE])
        uw = ring("uw", [P, U, F])
        sel = ring("sel", [P, U, P])
        eaT = ring("eaT", [P, U, L // 2, P])
        nuT = ring("nuT", [P, U, P])
        rp = ring("rp", [P, U, L, P])
        half = ring("half", [P, U, 2, P])
        rsum = ring("rsum", [P, U, P])
        mred = ring("mred", [P, U, P])
        smax = ring("smax", [P, U, P])
        ssum = ring("ssum", [P, U, P])
        rT = ring("rT", [P, U, 2 * P])
        ea_in = [sem(f"ea_in{k}") for k in range(U)]
        uw_in = [sem(f"uw_in{k}") for k in range(U)]
        rows_out = [sem(f"rows_out{k}") for k in range(U)]
        idx_done = sem("idx_done")
        turned = sem("turned")
        eaT_done = sem("eaT_done")
        z_done = sem("z_done")
        rp_done = sem("rp_done")
        half_done = sem("half_done")
        rsum_done = sem("rsum_done")
        m_done = sem("m_done")
        mask_done = sem("mask_done")
        spread_done = sem("spread_done")
        sel_done = sem("sel_done")
        mred_done = sem("mred_done")
        scan_done = sem("scan_done")
        r_turned = sem("r_turned")
        rT_done = sem("rT_done")

        AHEAD = 3

        def upto_last(t):
            return min(t, T) if isinstance(t, int) else t

        with nc.Block() as block:
            @block.gpsimd
            def _(pool):
                def take_index(i, k):
                    t = U * i + k
                    if not (isinstance(i, int) and i == 0):
                        pool.wait_ge(ea_in[k], 16 * i)
                    nc.gpsimd.tensor_copy(idx[:, k, :], s_index[:, bass.ds(t, 1)]).then_inc(idx_done, 1)

                def gather(i, k):
                    t = U * i + k
                    at_least(pool, idx_done, t + 1)
                    at_least(pool, turned, t - U + 1, alone=True)
                    pool.indirect_dma_start(
                        out=ea[:, k, :], out_offset=None, in_=chunk_rows,
                        in_offset=bass.IndirectOffsetOnAxis(ap=idx[:, k, :], axis=0)
                    ).then_inc(ea_in[k], 16)

                def sum_edges(i, k):
                    t = U * i + k
                    at_least(pool, rp_done, t + 1)
                    nc.gpsimd.tensor_tensor(half[:, k, :, :], rp[:, k, 0:2, :], rp[:, k, 2:4, :],
                                            ALU.add).then_inc(half_done, 1)
                    at_least(pool, half_done, t + 1)
                    at_least(pool, scan_done, t - U + 1)
                    nc.gpsimd.tensor_tensor(rsum[:, k, :], half[:, k, 0, :], half[:, k, 1, :],
                                            ALU.add).then_inc(rsum_done, 1)
                rolled(pool, T, [(take_index, 4), (sum_edges, 0), (gather, 4)])

            @block.tensor
            def _(pe):
                def spread(i, k):
                    t = U * i + k
                    at_least(pe, scan_done, t - 5)
                    at_least(pe, sel_done, t)
                    nc.tensor.matmul(ps_mask[:, 2 * P:3 * P], s_rel[:, bass.ds(t, 1)].broadcast_to([P, P]),
                                     identb[:, :], start=True, stop=True).then_inc(spread_done, 1)

                def turn(i, k):
                    t = U * i + k
                    pe.wait_ge(ea_in[k], 16 * i + 16)
                    pe.wait_ge(uw_in[k], 16 * i + 16)
                    at_least(pe, sel_done, t + 1)
                    at_least(pe, eaT_done, t - 1)
                    nc.tensor.transpose(ps_t[k % 2][:, 0:P], ea[:, k, 0:P], ident[:, :])
                    nc.tensor.transpose(ps_t[k % 2][:, P:2 * P], ea[:, k, P:2 * P], ident[:, :])
                    nc.tensor.matmul(ps_t[k % 2][:, 2 * P:3 * P], uw[:, k, :], sel[:, k, :], start=True,
                                     stop=True).then_inc(turned, 1)

                def drop_others(t, out):
                    for l in range(L):
                        last = nc.tensor.matmul(out[:, l * P:(l + 1) * P],
                                                inv[:, bass.ds(t, 1), l].broadcast_to([P, P]),
                                                neg_ident[:, :], start=False, stop=l == L - 1,
                                                skip_group_check=True)
                    return last

                def edge_product(i, k):
                    t = U * i + k
                    at_least(pe, eaT_done, t + 1)
                    at_least(pe, rp_done, t - 1)
                    z = ps_z[k % 2].rearrange("f (j r s) -> f j r s", j=L // 2, r=2)
                    for r in range(2):
                        nc.tensor.matmul(z[:, :, r, :], w1b[:, r, :], eaT[:, k, :, :], start=r == 0, stop=False,
                                         skip_group_check=True)
                    drop_others(t, ps_z[k % 2]).then_inc(z_done, 1)

                def message(i, k):
                    t = U * i + k
                    at_least(pe, rp_done, t + 1)
                    at_least(pe, mred_done, t - 1)
                    nc.tensor.matmul(ps_m[k % 2][:, :], w2[:, :], rp[:, k, :, :], start=True, stop=False,
                                     skip_group_check=True)
                    drop_others(t, ps_m[k % 2]).then_inc(m_done, 1)

                def masks(i, k):
                    t = U * i + k
                    at_least(pe, scan_done, t)
                    at_least(pe, sel_done, upto_last(t + AHEAD + 2))
                    nc.tensor.matmul(ps_mask[:, 0:P], starts[:, bass.ds(t, 1)].broadcast_to([P, P]),
                                     neg_ident[:, :], start=True, stop=True)
                    nc.tensor.matmul(ps_mask[:, P:2 * P], goes_on[:, bass.ds(t, 1)].broadcast_to([P, P]),
                                     identb[:, :], start=True, stop=True).then_inc(mask_done, 1)

                def turn_scans(i, k):
                    t = U * i + k
                    at_least(pe, scan_done, t + 1)
                    at_least(pe, rT_done, t)
                    nc.tensor.transpose(ps_r[:, 0:P], smax[:, k, :], ident[:, :])
                    nc.tensor.transpose(ps_r[:, P:2 * P], ssum[:, k, :], ident[:, :]).then_inc(r_turned, 1)
                rolled(pe, T, [(masks, -2), (spread, AHEAD), (turn, 1), (edge_product, 0), (message, -1),
                               (turn_scans, -3)])

            @block.scalar
            def _(act):
                def take_turned(i, k):
                    t = U * i + k
                    at_least(act, turned, t + 1)
                    at_least(act, z_done, t - U + 1)
                    at_least(act, rp_done, t - U + 1)
                    nc.scalar.activation(eaT[:, k, :, :], ps_t[k % 2][:, 0:2 * P], ACT.Copy)
                    nc.scalar.activation(nuT[:, k, :], ps_t[k % 2][:, 2 * P:3 * P], ACT.Copy,
                                         scale=-1.0).then_inc(eaT_done, 1)

                def take_rows(i, k):
                    t = U * i + k
                    at_least(act, r_turned, t + 1)
                    at_least(act, rows_out[k], 16 * i)
                    nc.scalar.activation(rT[:, k, :], ps_r[:, 0:2 * P], ACT.Copy).then_inc(rT_done, 1)
                rolled(act, T, [(take_turned, 1), (take_rows, -3)])

            @block.sync
            def _(sp):
                def load_u(i, k):
                    t = U * i + k
                    at_least(sp, turned, t - U + 1)
                    first = sp.value_load(base_i[0:1, bass.ds(t, 1)], min_val=0, max_val=NPP * P - P)
                    sp.dma_start(uw[:, k, :], utab[bass.ds(first, P), :]).then_inc(uw_in[k], 16)

                def store(i, k):
                    t = U * i + k
                    at_least(sp, rT_done, t + 1)
                    sp.dma_start(rtab[bass.ds(t * P, P), :], rT[:, k, :]).then_inc(rows_out[k], 16)
                rolled(sp, T, [(load_u, 3), (store, -3)])
                for k in range(U):
                    sp.wait_ge(rows_out[k], 16 * ((T - k + U - 1) // U))

            @block.vector
            def _(dve):
                v = nc.vector

                def select_nodes(i, k):
                    t = U * i + k
                    at_least(dve, spread_done, t + 1)
                    at_least(dve, turned, t - U + 1)
                    v.tensor_scalar(sel[:, k, :], ps_mask[:, 2 * P:3 * P], row[:, :], None,
                                    ALU.is_equal).then_inc(sel_done, 1)

                def relu_less_u(i, k):
                    t = U * i + k
                    at_least(dve, z_done, t + 1)
                    at_least(dve, m_done, t - U + 1)
                    at_least(dve, rsum_done, t - U + 1)
                    v.tensor_tensor(rp[:, k, :, :], ps_z[k % 2].rearrange("f (l s) -> f l s", l=L),
                                    nuT[:, k:k + 1, :].broadcast_to([P, L, P]), ALU.max).then_inc(rp_done, 1)

                def reduce_message(i, k):
                    t = U * i + k
                    at_least(dve, m_done, t + 1)
                    at_least(dve, scan_done, t - U + 1)
                    v.tensor_reduce(mred[:, k, :], ps_m[k % 2].rearrange("f (l s) -> f s l", l=L), AX.X,
                                    ALU.max).then_inc(mred_done, 1)

                def scan(i, k):
                    t = U * i + k
                    at_least(dve, rsum_done, t + 1)
                    at_least(dve, mask_done, t + 1)
                    at_least(dve, spread_done, upto_last(t + AHEAD + 3))
                    at_least(dve, mred_done, t + 1)
                    at_least(dve, scan_done, t)
                    at_least(dve, r_turned, t - U + 1)
                    first, before = isinstance(t, int) and t == 0, (k - 1) % U
                    v.tensor_tensor_scan(out=ssum[:, k, :], data0=ps_mask[:, P:2 * P], data1=rsum[:, k, :],
                                         initial=0.0 if first else ssum[:, before, P - 1:P], op0=ALU.mult,
                                         op1=ALU.add)
                    v.tensor_tensor_scan(out=smax[:, k, :], data0=ps_mask[:, 0:P], data1=mred[:, k, :],
                                         initial=-BIG if first else smax[:, before, P - 1:P], op0=ALU.add,
                                         op1=ALU.max).then_inc(scan_done, 1)
                rolled(dve, T, [(select_nodes, AHEAD), (scan, -2), (relu_less_u, 0), (reduce_message, -1)])

        stage.close()
        rg = ring("rg", [P, U, 2 * F])
        ridx = ring("ridx", [P, U, 1], I32)
        su = ring("su", [P, U, 2, F])
        suT = ring("suT", [P, U, 2, P])
        ag = ring("ag", [P, U, 2, F])
        agT = ring("agT", [P, U, 2, P])
        rm = ring("rm", [P, U, F])
        ob = ring("ob", [P, U, F])

        rg_in = [sem(f"rg_in{k}") for k in range(U)]
        ridx_done = sem("ridx_done")
        bias_done = sem("bias_done")
        su_done = sem("su_done")
        uc_done = sem("uc_done")
        su_turned = sem("su_turned")
        suT_done = sem("suT_done")
        sw_done = sem("sw_done")
        rm_done = sem("rm_done")
        ag_done = sem("ag_done")
        ag_turned = sem("ag_turned")
        agT_done = sem("agT_done")
        o_done = sem("o_done")
        o_mid = sem("o_mid")
        o_ready = sem("o_ready")
        out_out = sem("out_out")
        ps_s, ps_g, ps_a, ps_o = bank[0:2], bank[2:4], bank[4:6], bank[6:8]

        with nc.Block() as block:
            @block.gpsimd
            def _(pool):
                def gather(i, k):
                    b = U * i + k
                    if not (isinstance(i, int) and i == 0):
                        pool.wait_ge(rg_in[k], 16 * i)
                    nc.gpsimd.tensor_copy(ridx[:, k, :], gendi[:, bass.ds(b, 1)]).then_inc(ridx_done, 1)
                    at_least(pool, ridx_done, b + 1)
                    at_least(pool, ag_done, b - U + 1, alone=True)
                    pool.indirect_dma_start(
                        out=rg[:, k, :], out_offset=None, in_=rtab,
                        in_offset=bass.IndirectOffsetOnAxis(ap=ridx[:, k, :], axis=0)
                    ).then_inc(rg_in[k], 16)
                rolled(pool, NPP, [(gather, 0)])

            @block.scalar
            def _(act):
                def copy_u(i, k):
                    b = U * i + k
                    at_least(act, su_turned, b - U + 1)
                    nc.scalar.activation(su[:, k, 1, :], us[:, bass.ds(b, 1), :], ACT.Copy).then_inc(uc_done, 1)

                def take_su(i, k):
                    b = U * i + k
                    at_least(act, su_turned, b + 1)
                    at_least(act, sw_done, b - U + 1)
                    nc.scalar.activation(suT[:, k, :, :], ps_s[k % 2][:, 0:2 * P], ACT.Copy).then_inc(suT_done, 1)

                def take_ag(i, k):
                    b = U * i + k
                    at_least(act, ag_turned, b + 1)
                    at_least(act, o_done, b - U + 1)
                    nc.scalar.activation(agT[:, k, :, :], ps_a[k % 2][:, 0:2 * P], ACT.Copy).then_inc(agT_done, 1)
                def drop_empty(i, k):
                    b = U * i + k
                    act.wait_ge(rg_in[k], 16 * i + 16)
                    at_least(act, ag_done, b - U + 1)
                    nc.scalar.activation(rm[:, k, :], rg[:, k, 0:F], ACT.Copy,
                                         scale=some[:, bass.ds(b, 1)]).then_inc(rm_done, 1)
                rolled(act, NPP, [(take_su, 1), (copy_u, 3), (drop_empty, 1), (take_ag, -1)])

            @block.tensor
            def _(pe):
                def turn_su(i, k):
                    b = U * i + k
                    at_least(pe, su_done, b + 1)
                    at_least(pe, uc_done, b + 1)
                    at_least(pe, suT_done, b - 1)
                    nc.tensor.transpose(ps_s[k % 2][:, 0:P], su[:, k, 0, :], ident[:, :])
                    nc.tensor.transpose(ps_s[k % 2][:, P:2 * P], su[:, k, 1, :], ident[:, :]).then_inc(su_turned, 1)

                def by_w2(i, k):
                    b = U * i + k
                    at_least(pe, suT_done, b + 1)
                    at_least(pe, ag_done, b - 1)
                    nc.tensor.matmul(ps_g[k % 2][:, 0:F], suT[:, k, 0, :], w2[:, :], start=True, stop=True)
                    nc.tensor.matmul(ps_g[k % 2][:, F:2 * F], suT[:, k, 1, :], w2[:, :], start=True, stop=False)
                    nc.tensor.matmul(ps_g[k % 2][:, F:2 * F], ones[0:1, :], b2r[0:1, :], start=False,
                                     stop=True).then_inc(sw_done, 1)

                def turn_ag(i, k):
                    b = U * i + k
                    at_least(pe, ag_done, b + 1)
                    at_least(pe, agT_done, b - 1)
                    nc.tensor.transpose(ps_a[k % 2][:, 0:P], ag[:, k, 0, :], ident[:, :])
                    nc.tensor.transpose(ps_a[k % 2][:, P:2 * P], ag[:, k, 1, :], ident[:, :]).then_inc(ag_turned, 1)

                def outputs(i, k):
                    b = U * i + k
                    at_least(pe, agT_done, b + 1)
                    at_least(pe, o_ready, b - 1)
                    nc.tensor.matmul(ps_o[k % 2][:, 0:F], agT[:, k, 0, :], ws[:, :], start=True, stop=False)
                    nc.tensor.matmul(ps_o[k % 2][:, 0:F], agT[:, k, 1, :], wx[:, :], start=False, stop=True)
                    nc.tensor.matmul(ps_o[k % 2][:, F:2 * F], agT[:, k, 0, :], wm[:, :], start=True,
                                     stop=True).then_inc(o_done, 1)
                rolled(pe, NPP, [(turn_su, 2), (by_w2, 0), (turn_ag, -1), (outputs, -2)])

            @block.vector
            def _(dve):
                v = nc.vector
                v.tensor_tensor(bor[:, 0, :], bor[:, 0, :], bor[:, 1, :], ALU.add).then_inc(bias_done, 1)
                dve.wait_ge(bias_done, 1)
                v.tensor_tensor(bor[:, 0, :], bor[:, 0, :], bor[:, 2, :], ALU.add).then_inc(bias_done, 1)
                dve.wait_ge(bias_done, 2)
                v.tensor_tensor(xs[:, :, :], xs[:, :, :], bor[:, 0:1, :].broadcast_to([P, NPP, F]),
                                ALU.add).then_inc(bias_done, 1)
                dve.wait_ge(bias_done, 3)

                def sum_relu(i, k):
                    b = U * i + k
                    dve.wait_ge(rg_in[k], 16 * i + 16)
                    at_least(dve, su_turned, b - U + 1)
                    v.scalar_tensor_tensor(su[:, k, 0, :], us[:, bass.ds(b, 1), :], slots_l[:, bass.ds(b, 1)],
                                           rg[:, k, F:2 * F], ALU.mult, ALU.add).then_inc(su_done, 1)

                def with_bias(i, k):
                    b = U * i + k
                    at_least(dve, ag_turned, b - U + 1)
                    at_least(dve, sw_done, b + 1)
                    v.scalar_tensor_tensor(ag[:, k, 0, :], b2r[:, :], count[:, bass.ds(b, 1)], ps_g[k % 2][:, 0:F],
                                           ALU.mult, ALU.add)
                    at_least(dve, rm_done, b + 1)
                    v.scalar_tensor_tensor(ag[:, k, 1, :], ps_g[k % 2][:, F:2 * F], some[:, bass.ds(b, 1)],
                                           rm[:, k, :], ALU.mult, ALU.add).then_inc(ag_done, 1)

                def finish(i, k):
                    b = U * i + k
                    at_least(dve, o_done, b + 1)
                    v.scalar_tensor_tensor(ob[:, k, :], ps_o[k % 2][:, F:2 * F], rcount[:, bass.ds(b, 1)],
                                           xs[:, bass.ds(b, 1), :], ALU.mult, ALU.add).then_inc(o_mid, 1)

                def finish_sum(i, k):
                    b = U * i + k
                    at_least(dve, o_mid, b + 1)
                    v.tensor_tensor(xs[:, bass.ds(b, 1), :], ob[:, k, :], ps_o[k % 2][:, 0:F],
                                    ALU.add).then_inc(o_ready, 1)
                rolled(dve, NPP, [(with_bias, 0), (sum_relu, 3), (finish, -3), (finish_sum, -3)])

            @block.sync
            def _(sp):
                sp.wait_ge(o_ready, NPP)
                for p0, p1, nb, rows in node_rows(out):
                    sp.dma_start(rows, xs[p0:p1, 0:nb, :]).then_inc(out_out, 16)
                sp.wait_ge(out_out, 16 * 3)


_INS = ["x", "dst", "edge_attr_64", "L0_gnn_W1", "L0_gnn_b1", "L0_gnn_W2", "L0_gnn_b2", "L0_gnn_Wm", "L0_gnn_bm",
        "L0_gnn_Wx", "L0_gnn_bx", "L0_gnn_Ws", "L0_gnn_bs"]


def kernel(**inputs):
    import numpy as np

    import concourse.bacc as bacc
    from concourse.bass_utils import run_bass_kernel_spmd

    nc = bacc.Bacc("TRN2", target_bir_lowering=False, num_devices=1)
    arrays, args = {}, []
    for name in _INS:
        a = np.ascontiguousarray(inputs[name])
        arrays[f"in_{name}"] = a
        args.append(nc.dram_tensor(f"in_{name}", a.shape, mybir.dt.from_np(a.dtype), kind="ExternalInput").ap())
    args.append(nc.dram_tensor("out_0", inputs["x"].shape, F32, kind="ExternalOutput").ap())
    gnn_kernel(nc, *args)
    r = run_bass_kernel_spmd(nc, [arrays], core_ids=[0])
    return r.results[0]["out_0"]
```

```python
from contextlib import ExitStack

import concourse.bass as bass
from concourse import mybir

F32 = mybir.dt.float32
BF16 = mybir.dt.bfloat16
I32 = mybir.dt.int32
U8 = mybir.dt.uint8
ALU = mybir.AluOpType
ACT = mybir.ActivationFunctionType
AX = mybir.AxisListType

P = 128
BIG = 1e30
EPS = 1e-5


def at_least(engine, semaphore, value, alone=False):
    if isinstance(value, int) and value <= 0:
        return
    engine.wait_ge(semaphore, value)
    if alone:
        engine.nop(nofuse=True)


U = 4


def rolled(engine, n, order):
    least, most = min(o for _, o in order), max(o for _, o in order)
    first = -(least // U) * U + U
    last = n - most
    last -= (last - first) % U

    def at(t):
        for step, o in order:
            if 0 <= t + o < n:
                step((t + o) // U, (t + o) % U)
    for t in range(-most, first):
        at(t)
    with engine.Fori(first // U, last // U) as i:
        for k in range(U):
            for step, o in order:
                step(i + (k + o) // U, (k + o) % U)
    for t in range(last, n - least):
        at(t)


def gnn_kernel(nc, x, dst, edge, W1, b1, W2, b2, Wm, bm, Wx, bx, Ws, bs, out):
    N, F = x.shape
    E, FE = edge.shape
    assert F == P and 2 * FE == P
    L = 4
    NPP = -(-N // P)
    FULL = N // NPP
    REST = N - FULL * NPP
    EVEN = FULL // 16 * 16
    CHUNKS = E // L
    T = -(-(CHUNKS + NPP * P) // P)
    PREP = T // U
    BS = 250
    NB = E // BS
    assert FULL == P - 1 and E % BS == 0 and E % L == 0 and T <= 256 and NPP <= PREP

    utab = nc.dram_tensor("utab", (NPP * P, F), F32, kind="Internal").ap()
    rtab = nc.dram_tensor("rtab", (T * P, 2 * F), F32, kind="Internal").ap()
    MASKS = 2 * 2 * P
    ROW = MASKS + L * P
    mtab = nc.dram_tensor("mtab", (T, ROW), U8, kind="Internal").ap()
    ntab = nc.dram_tensor("ntab", (T, P), BF16, kind="Internal").ap()
    chunk_rows = edge.rearrange("(c l) f -> c (l f)", l=L)
    search_rows = dst.rearrange("(a b) -> a b", b=BS)

    def node_rows(a):
        whole = a[0:FULL * NPP, :].rearrange("(p b) f -> p b f", b=NPP)
        return ((0, EVEN, NPP, whole[0:EVEN]), (EVEN, FULL, NPP, whole[EVEN:FULL]),
                (FULL, FULL + 1, REST, a[FULL * NPP:N, :].rearrange("(p b) f -> p b f", b=REST)))

    with ExitStack() as ctx:
        def sb(name, shape, dt=F32):
            return ctx.enter_context(nc.sbuf_tensor(name, shape, dt))

        def sem(name):
            return ctx.enter_context(nc.semaphore(name))

        bank = [ctx.enter_context(nc.psum_tensor(f"bank{i}", [P, 512], F32)) for i in range(8)]
        ps_z, ps_m, ps_t, ps_mask, ps_r = bank[0:2], bank[2:4], bank[4:6], bank[6], bank[7]

        ident = sb("ident", [P, P])
        identb = sb("identb", [P, P], BF16)
        neg_ident = sb("neg_ident", [P, P], BF16)
        onesb = sb("onesb", [P, P], BF16)
        ones = sb("ones", [P, P])
        tri = sb("tri", [P, P], BF16)
        next_lane = sb("next_lane", [P, P], BF16)
        next_tile = sb("next_tile", [P, P], BF16)
        iota_i = sb("iota_i", [P, 256], I32)
        iotab = sb("iotab", [P, 256], BF16)
        w1u = sb("w1u", [P, 2, F])
        w1b = sb("w1b", [P, 2, F])
        w2 = sb("w2", [P, F])
        wo = sb("wo", [P, 3, F])
        w2o = sb("w2o", [P, 3, F])
        w_turned = sb("w_turned", [P, 2, P])
        b1uv = sb("b1uv", [P, 2, F])
        b12 = sb("b12", [P, 2])
        b2s = sb("b2s", [P, 1, F])
        bor = sb("bor", [P, 3, F])
        xs = sb("xs", [P, PREP, F])
        uv = sb("uv", [P, PREP, 2, F])
        nodei = sb("nodei", [P, NPP + 1], I32)
        nodef = sb("nodef", [P, NPP + 1])
        stats = sb("stats", [P, NPP, 6])
        mv = sb("mv", [P, NPP, 2])
        sd = sb("sd", [P, 4, NPP])
        rstd = sb("rstd", [P, NPP])
        shift = sb("shift", [P, NPP])
        coarse = sb("coarse", [P, NPP + 1])
        coarse_i = sb("coarse_i", [P, NPP + 1], I32)
        fine = sb("fine", [P, NPP + 1])
        start = sb("start", [P, NPP + 1])
        count = sb("count", [P, PREP])
        rcount = sb("rcount", [P, NPP])
        some = sb("some", [P, PREP])
        edge_i = sb("edge_i", [P, 2, NPP], I32)
        edge_f = sb("edge_f", [P, 2, NPP])
        chunk_i = sb("chunk_i", [P, 2, NPP], I32)
        chunk_f = sb("chunk_f", [P, 2, NPP])
        place_i = sb("place_i", [P, NPP], I32)
        slot_f = sb("slot_f", [P, 2, NPP])
        slot_i = sb("slot_i", [P, 2, NPP], I32)
        tile_i = sb("tile_i", [P, NPP], I32)
        tile_f = sb("tile_f", [P, NPP])
        lane_i = sb("lane_i", [P, NPP], I32)
        lane_f = sb("lane_f", [P, NPP])
        mark = sb("mark", [P, NPP])
        slots_l = sb("slots_l", [P, NPP])
        others = sb("others", [P, NPP])
        slotf = sb("slotf", [P, T])
        sloti = sb("sloti", [P, T], I32)
        starts = sb("starts", [P, T], BF16)
        goes_on = sb("goes_on", [P, T], BF16)
        before = sb("before", [P, T + 1], BF16)
        kept = sb("kept", [P, T])
        total = sb("total", [P, T])
        zeros = sb("zeros", [P, T])
        upto = sb("upto", [P, T])
        s_node = sb("s_node", [P, T])
        s_index = sb("s_index", [P, T], I32)
        late = sb("late", [P, T, L], BF16)
        inv = sb("inv", [P, T, L], BF16)
        own = sb("own", [P, T, L])
        base_i = sb("base_i", [1, T], I32)
        row = sb("row", [P, 1])
        row_i = sb("row_i", [P, 1], I32)
        stage = ctx.enter_context(ExitStack())

        def ring(name, shape, dt=F32):
            return stage.enter_context(nc.sbuf_tensor(name, shape, dt))

        last_i = ring("last_i", [1, NB], I32)
        last_f = ring("last_f", [1, NB])
        lasts = ring("lasts", [P, NB])
        half_less_node = ring("half_less_node", [P, NPP + 1])
        signs = ring("signs", [P, NPP + 1])
        junk = ring("junk", [P, U, NB], BF16)
        junk2 = ring("junk2", [P, U, NB], BF16)
        tile_hot = ring("tile_hot", [P, U, T], BF16)
        hn = ring("hn", [P, U, F])
        hT = ring("hT", [P, U, F])
        found = ring("found", [P, NPP + 1, BS], I32)
        lane_hot = ring("lane_hot", [P, U, P], BF16)
        mrows = ring("mrows", [P, 2, ROW], U8)
        nrows = ring("nrows", [P, 2, P], BF16)
        first_node = ring("first_node", [P, 2])
        x_in = sem("x_in")
        w_in = sem("w_in")
        last_in = sem("last_in")
        zeroed = sem("zeroed")
        const_done = sem("const_done")
        pool_chain = sem("pool_chain")
        dve_chain = sem("dve_chain")
        lasts_ready = sem("lasts_ready")
        lasts_bc = sem("lasts_bc")
        lasts_done = sem("lasts_done")
        coarse_step = sem("coarse_step")
        signs_step = sem("signs_step")
        coarse_done = sem("coarse_done")
        found_in = [sem(f"found_in{k}") for k in range(U)]
        fine_step = sem("fine_step")
        stats_done = sem("stats_done")
        var_done = sem("var_done")
        sd_done = sem("sd_done")
        rstd_done = sem("rstd_done")
        w_step = sem("w_step")
        wT_done = sem("wT_done")
        w2o_done = sem("w2o_done")
        w1u_done = sem("w1u_done")
        h_done = sem("h_done")
        h_turned = sem("h_turned")
        hT_done = sem("hT_done")
        uv_done = sem("uv_done")
        uv_read = sem("uv_read")
        goes_on_done = sem("goes_on_done")
        before_done = sem("before_done")
        next_before = sem("next_before")
        masks_turned = sem("masks_turned")
        inv_done = sem("inv_done")
        inv_turned = sem("inv_turned")
        mrows_done = sem("mrows_done")
        mtab_out = sem("mtab_out")
        hot_done = sem("hot_done")
        hot_used = sem("hot_used")
        starts_done = sem("starts_done")
        prefix_done = sem("prefix_done")
        s_node_done = sem("s_node_done")
        nodes_turned = sem("nodes_turned")
        first_done = sem("first_done")
        nrows_done = sem("nrows_done")
        ntab_out = sem("ntab_out")
        utab_out = sem("utab_out")
        chain = [0]

        def link(dve, instruction):
            chain[0] += 1
            instruction.then_inc(dve_chain, 1)
            dve.wait_ge(dve_chain, chain[0])

        HALF = (NPP + 3) // 2
        X_DMAS, W_DMAS = 3, 13
        TILE_GROUPS = ((0, P), (P, T - P))
        ps_uv = bank[0:4]
        with nc.Block() as block:
            @block.sync
            def _(sp):
                sp.dma_start(last_i[:, :], search_rows[:, BS - 1:BS].rearrange("a b -> b a"),
                             allow_slow_non_contiguous=True).then_inc(last_in, 16)
                sp.wait_ge(zeroed, 1)
                for p0, p1, nb, rows in node_rows(x):
                    sp.dma_start(xs[p0:p1, 0:nb, :], rows).then_inc(x_in, 16)
                sp.dma_start(w1u[:, 0, :], W1[0:F, :]).then_inc(w_in, 16)
                sp.dma_start(w2[:, :], W2).then_inc(w_in, 16)
                for o, a in enumerate((Ws, Wm, Wx)):
                    sp.dma_start(wo[:, o, :], a).then_inc(w_in, 16)
                for o, a in enumerate((b1, b2)):
                    sp.dma_start(b12[:, o:o + 1], a.rearrange("(f a) -> f a", a=1)).then_inc(w_in, 16)
                for t, a in ((b1uv[:, 0, :], b1), (bor[:, 0, :], bm), (bor[:, 1, :], bx), (bor[:, 2, :], bs)):
                    sp.dma_start(t, a.rearrange("(a f) -> a f", a=1).broadcast_to([P, F])).then_inc(w_in, 16)
                sp.dma_start(w1b[0:FE, 0, :], W1[F:F + FE, :]).then_inc(w_in, 16)
                sp.dma_start(w1b[FE:P, 1, :], W1[F:F + FE, :]).then_inc(w_in, 16)
                sp.wait_ge(uv_read, NPP)
                sp.dma_start(utab.rearrange("(p b) f -> p b f", b=NPP), uv[:, 0:NPP, 0, :]).then_inc(utab_out, 16)
                for g, (t0, n) in enumerate(TILE_GROUPS):
                    sp.wait_ge(nrows_done, g + 1)
                    sp.dma_start(ntab[t0:t0 + n, :], nrows[0:n, g, :]).then_inc(ntab_out, 16)
                for g, (t0, n) in enumerate(TILE_GROUPS):
                    sp.wait_ge(mrows_done, g + 1)
                    sp.dma_start(mtab[t0:t0 + n, :], mrows[0:n, g, :]).then_inc(mtab_out, 16)
                sp.wait_ge(utab_out, 16)

            @block.scalar
            def _(act):
                act.wait_ge(lasts_done, 1)

                def add_signs(i, k):
                    j = U * i + k
                    b = bass.ds(j + HALF, 1)
                    at_least(act, signs_step, j - 1)
                    nc.scalar.activation(junk2[:, k, :], lasts[:, :], ACT.Sign, bias=half_less_node[:, b],
                                         accum_out=signs[:, b]).then_inc(signs_step, 1)
                rolled(act, NPP + 1 - HALF, [(add_signs, 0)])

                act.wait_ge(w_step, 1)
                nc.scalar.activation(w_turned[:, :, :], ps_r[:, 0:2 * P], ACT.Copy).then_inc(wT_done, 1)
                act.wait_ge(w_step, 2)
                nc.scalar.activation(w2o[:, :, :], ps_z[1][:, 0:3 * F], ACT.Copy).then_inc(w2o_done, 1)
                act.wait_ge(w_step, 3)
                nc.scalar.activation(w1u[:, 1, :], ps_r[:, 0:F], ACT.Copy)
                nc.scalar.activation(b1uv[:, 1, :], ps_r[:, F:2 * F], ACT.Copy)
                nc.scalar.activation(b2s[:, 0, :], ps_r[:, 2 * F:3 * F], ACT.Copy).then_inc(w1u_done, 1)

                act.wait_ge(var_done, 1)
                nc.scalar.activation(sd[:, 0, :], sd[:, 1, :], ACT.Sqrt).then_inc(sd_done, 1)
                act.wait_ge(rstd_done, 1)

                def normalise(i, k):
                    b = U * i + k
                    at_least(act, h_turned, b - U + 1)
                    nc.scalar.activation(hn[:, k, :], xs[:, bass.ds(b, 1), :], ACT.Relu, scale=rstd[:, bass.ds(b, 1)],
                                         bias=shift[:, bass.ds(b, 1)]).then_inc(h_done, 1)

                def take_h(i, k):
                    b = U * i + k
                    at_least(act, h_turned, b + 1)
                    at_least(act, uv_done, b - U + 1)
                    nc.scalar.activation(hT[:, k, :], ps_t[k % 2][:, 0:F], ACT.Copy).then_inc(hT_done, 1)

                rolled(act, NPP, [(take_h, 1), (normalise, 3)])
                act.wait_ge(masks_turned, 1)
                for g, (t0, n) in enumerate(TILE_GROUPS):
                    nc.scalar.activation(mrows[0:n, g, 0:MASKS].bitcast(BF16), ps_t[g][0:n, 0:2 * P], ACT.Copy)
                act.wait_ge(inv_turned, 1)
                for g, (t0, n) in enumerate(TILE_GROUPS):
                    nc.scalar.activation(mrows[0:n, g, MASKS:ROW], ps_uv[2 + g][0:n, :], ACT.Copy).then_inc(mrows_done, 1)

            @block.gpsimd
            def _(pool):
                nc.gpsimd.iota(nodei[:, :], pattern=[[1, NPP + 1]], base=0, channel_multiplier=NPP)
                nc.gpsimd.memset(ones[:, :], 1.0).then_inc(const_done, 1)
                nc.gpsimd.memset(xs[:, REST:PREP, :], 0.0)
                nc.gpsimd.memset(w1b[:, :, :], 0.0).then_inc(zeroed, 1)
                nc.gpsimd.iota(iota_i[:, :], pattern=[[1, 256]], base=0, channel_multiplier=0)
                nc.gpsimd.iota(sloti[:, :], pattern=[[P, T]], base=0, channel_multiplier=1)
                nc.gpsimd.memset(ident[:, :], 0.0)
                nc.gpsimd.memset(identb[:, :], 0.0)
                nc.gpsimd.memset(neg_ident[:, :], 0.0)
                nc.gpsimd.memset(onesb[:, :], 1.0)
                nc.gpsimd.memset(next_lane[:, :], 0.0)
                nc.gpsimd.memset(next_tile[:, :], 0.0)
                nc.gpsimd.memset(before[:, T:T + 1], 0.0)
                nc.gpsimd.iota(row_i[:, :], pattern=[[1, 1]], base=0, channel_multiplier=1)
                nc.gpsimd.memset(zeros[:, :], 0.0)
                nc.gpsimd.memset(uv[:, NPP:PREP, :, :], 0.0)
                nc.gpsimd.memset(count[:, NPP:PREP], 0.0)
                nc.gpsimd.memset(some[:, NPP:PREP], 0.0)
                nc.gpsimd.memset(tri[:, :], 1.0).then_inc(pool_chain, 1)
                pool.wait_ge(pool_chain, 1)
                for m, v, above in ((ident, 1.0, 0), (identb, 1.0, 0), (neg_ident, -BIG, 0), (next_lane, 1.0, -1),
                                    (next_tile, 1.0, P - 1)):
                    nc.gpsimd.affine_select(out=m[:, :], in_=m[:, :], compare_op=ALU.not_equal, fill=v, base=above,
                                            pattern=[[-1, P]], channel_multiplier=1)
                nc.gpsimd.affine_select(out=tri[:, :], in_=tri[:, :], compare_op=ALU.is_ge, fill=0.0, base=0,
                                        pattern=[[1, P]], channel_multiplier=-1).then_inc(const_done, 1)
                pool.wait_ge(coarse_done, 1)

                def find_block(i, k):
                    b = U * i + k
                    if not (isinstance(i, int) and i == 0):
                        pool.wait_ge(found_in[k], 16 * i)
                    pool.indirect_dma_start(
                        out=found[:, b, :], out_offset=None, in_=search_rows,
                        in_offset=bass.IndirectOffsetOnAxis(ap=coarse_i[:, b:b + 1], axis=0)
                    ).then_inc(found_in[k], 16)
                for b in range(NPP + 1):
                    find_block(b // U, b % U)

            @block.tensor
            def _(pe):
                pe.wait_ge(const_done, 1)
                pe.wait_ge(lasts_ready, 1)
                nc.tensor.matmul(ps_z[0][:, 0:NB], ones[0:1, :], last_f[0:1, :], start=True,
                                 stop=True).then_inc(lasts_bc, 1)
                pe.wait_ge(const_done, 2)
                pe.wait_ge(w_in, 16 * W_DMAS)
                nc.tensor.transpose(ps_r[:, 0:P], w2[:, :], ident[:, :])
                nc.tensor.transpose(ps_r[:, P:2 * P], w1u[:, 0, :], ident[:, :]).then_inc(w_step, 1)
                pe.wait_ge(wT_done, 1)
                nc.tensor.matmul(ps_z[1][:, 0:3 * F], w_turned[:, 0, :], wo[:, :, :], start=True,
                                 stop=True).then_inc(w_step, 1)
                pe.wait_ge(w2o_done, 1)
                b1_rows, b2_rows = (b12[:, o:o + 1].broadcast_to([P, P]) for o in range(2))
                nc.tensor.matmul(ps_r[:, 0:F], w_turned[:, 1, :], w2o[:, 2, :], start=True, stop=True)
                nc.tensor.matmul(ps_r[:, F:2 * F], b1_rows, w2o[:, 2, :], start=True, stop=False)
                nc.tensor.matmul(ps_r[:, F:2 * F], b2_rows, wo[:, 2, :], start=False, stop=False)
                nc.tensor.matmul(ps_r[:, F:2 * F], b2_rows, wo[:, 1, :], start=False, stop=True)
                nc.tensor.matmul(ps_r[:, 2 * F:3 * F], b2_rows, wo[:, 0, :], start=True,
                                 stop=True).then_inc(w_step, 1)
                pe.wait_ge(w1u_done, 1)

                def turn_h(i, k):
                    b = U * i + k
                    at_least(pe, h_done, b + 1)
                    at_least(pe, hT_done, b - 1)
                    nc.tensor.transpose(ps_t[k % 2][:, 0:F], hn[:, k, :], ident[:, :]).then_inc(h_turned, 1)

                def uv_product(i, k):
                    b = U * i + k
                    at_least(pe, hT_done, b + 1)
                    at_least(pe, uv_read, b - U + 1)
                    nc.tensor.matmul(ps_uv[k][:, 0:2 * F], hT[:, k, :], w1u[:, :, :], start=True,
                                     stop=True).then_inc(uv_done, 1)
                rolled(pe, NPP, [(turn_h, 2), (uv_product, 0)])

                def add_nodes(i, k):
                    b = U * i + k
                    at_least(pe, hot_done, b + 1)
                    is_int = isinstance(b, int)
                    nc.tensor.matmul(ps_mask[:, 0:T], lane_hot[:, k, :], tile_hot[:, k, :], start=is_int and b == 0,
                                     stop=is_int and b == NPP - 1).then_inc(hot_used, 1)
                rolled(pe, NPP, [(add_nodes, 0)])
                pe.wait_ge(starts_done, 1)
                nc.tensor.matmul(ps_r[:, 0:T], tri[:, :], starts[:, :], start=True, stop=True)
                nc.tensor.matmul(ps_r[:, 256:256 + T], onesb[:, :], starts[:, :], start=True,
                                 stop=True).then_inc(prefix_done, 1)
                pe.wait_ge(before_done, 1)
                pe.wait_ge(uv_read, NPP)
                nc.tensor.matmul(ps_z[0][:, 0:T], next_lane[:, :], before[:, 0:T], start=True, stop=False)
                nc.tensor.matmul(ps_z[0][:, 0:T], next_tile[:, :], before[:, 1:T + 1], start=False,
                                 stop=True).then_inc(next_before, 1)
                pe.wait_ge(goes_on_done, 1)
                for g, (t0, n) in enumerate(TILE_GROUPS):
                    nc.tensor.matmul(ps_t[g][0:n, 0:P], starts[:, t0:t0 + n], neg_ident[:, :], start=True, stop=True)
                    last = nc.tensor.matmul(ps_t[g][0:n, P:2 * P], goes_on[:, t0:t0 + n], identb[:, :], start=True,
                                            stop=True)
                last.then_inc(masks_turned, 1)
                pe.wait_ge(s_node_done, 1)
                for g, (t0, n) in enumerate(TILE_GROUPS):
                    nc.tensor.transpose(ps_z[1][0:n, g * P:(g + 1) * P], s_node[:, t0:t0 + n],
                                        ident[:, :]).then_inc(nodes_turned, 1)
                pe.wait_ge(inv_done, 1)
                for g, (t0, n) in enumerate(TILE_GROUPS):
                    for l in range(L):
                        last = nc.tensor.matmul(ps_uv[2 + g][0:n, l * P:(l + 1) * P], inv[:, t0:t0 + n, l],
                                                identb[:, :], start=True, stop=True)
                last.then_inc(inv_turned, 1)

            @block.vector
            def _(dve):
                v = nc.vector
                dve.wait_ge(last_in, 16)
                v.tensor_copy(last_f[:, :], last_i[:, :]).then_inc(lasts_ready, 1)
                dve.wait_ge(const_done, 1)
                link(dve, v.tensor_copy(nodef[:, :], nodei[:, :]))
                v.tensor_scalar(half_less_node[:, :], nodef[:, :], -1.0, 0.5, ALU.mult, ALU.add)
                dve.wait_ge(lasts_bc, 1)
                v.tensor_copy(lasts[:, :], ps_z[0][:, 0:NB]).then_inc(lasts_done, 1)
                dve.wait_ge(lasts_done, 1)

                def count_blocks(i, k):
                    b = U * i + k
                    at_least(dve, coarse_step, b - 1)
                    v.tensor_scalar(junk[:, k, :], lasts[:, :], nodef[:, bass.ds(b, 1)], 0.0, ALU.is_lt, ALU.add,
                                    accum_out=coarse[:, bass.ds(b, 1)]).then_inc(coarse_step, 1)
                rolled(dve, HALF, [(count_blocks, 0)])
                dve.wait_ge(signs_step, NPP + 1 - HALF)
                v.tensor_scalar(coarse[:, HALF:NPP + 1], signs[:, HALF:NPP + 1], -0.5, NB / 2, ALU.mult,
                                ALU.add).then_inc(coarse_step, 1)
                dve.wait_ge(coarse_step, HALF + 1)
                link(dve, v.tensor_scalar(coarse[:, :], coarse[:, :], float(NB - 1), None, ALU.min))
                v.tensor_copy(coarse_i[:, :], coarse[:, :]).then_inc(coarse_done, 1)

                dve.wait_ge(x_in, 16 * X_DMAS)

                for b in range(NPP):
                    last = v.bn_stats(stats[:, b, :], xs[:, b, :])
                last.then_inc(stats_done, 1)
                dve.wait_ge(stats_done, 1)
                for b in range(NPP):
                    last = v.bn_aggr(mv[:, b, :], stats[:, b, :])
                link(dve, last)
                v.tensor_scalar(sd[:, 1, :], mv[:, :, 1], EPS, None, ALU.add).then_inc(var_done, 1)
                dve.wait_ge(sd_done, 1)
                link(dve, v.reciprocal(sd[:, 2, :], sd[:, 0, :]))
                link(dve, v.tensor_tensor(sd[:, 3, :], sd[:, 1, :], sd[:, 2, :], ALU.mult))
                link(dve, v.tensor_tensor(sd[:, 2, :], sd[:, 3, :], sd[:, 0, :], ALU.add))
                link(dve, v.tensor_scalar(sd[:, 3, :], sd[:, 2, :], 0.5, None, ALU.mult))
                link(dve, v.reciprocal(rstd[:, :], sd[:, 3, :]))
                link(dve, v.tensor_tensor(shift[:, :], mv[:, :, 0], rstd[:, :], ALU.mult))
                v.tensor_scalar(shift[:, :], shift[:, :], -1.0, None, ALU.mult).then_inc(rstd_done, 1)
                v.tensor_copy(row[:, :], row_i[:, :])
                dve.wait_ge(const_done, 2)
                v.tensor_copy(iotab[:, :], iota_i[:, :])
                v.tensor_copy(slotf[:, :], sloti[:, :])
                dve.wait_ge(w_in, 16 * W_DMAS)
                link(dve, v.tensor_tensor(bor[:, 0, :], bor[:, 0, :], bor[:, 1, :], ALU.add))
                v.tensor_tensor(bor[:, 0, :], bor[:, 0, :], bor[:, 2, :], ALU.add)

                def add_b1(i, k):
                    at_least(dve, uv_done, U * i + k + 1)
                    v.tensor_tensor(uv[:, bass.ds(U * i + k, 1), :, :], ps_uv[k][:, 0:2 * F], b1uv[:, :, :],
                                    ALU.add).then_inc(uv_read, 1)

                def count_edges(i, k):
                    b = U * i + k
                    dve.wait_ge(found_in[k], 16 * i + 16)
                    at_least(dve, fine_step, b - 1)
                    v.tensor_scalar(junk[:, k, 0:BS], found[:, bass.ds(b, 1), :], nodef[:, bass.ds(b, 1)], 0.0,
                                    ALU.is_lt, ALU.add, accum_out=fine[:, bass.ds(b, 1)]).then_inc(fine_step, 1)
                dve.wait_ge(w1u_done, 1)
                rolled(dve, NPP, [(count_edges, 0), (add_b1, 0)])
                count_edges(NPP // U, NPP % U)
                dve.wait_ge(fine_step, NPP + 1)
                link(dve, v.scalar_tensor_tensor(start[:, :], coarse[:, :], float(BS), fine[:, :], ALU.mult,
                                                 ALU.add))
                first, end = start[:, 0:NPP], start[:, 1:NPP + 1]
                v.tensor_copy(edge_i[:, 0, :], first)
                link(dve, v.scalar_tensor_tensor(edge_f[:, 1, :], end, -1.0, first, ALU.add, ALU.max))
                link(dve, v.tensor_copy(edge_i[:, 1, :], edge_f[:, 1, :]))
                v.tensor_scalar(chunk_i[:, :, :], edge_i[:, :, :], (L - 1).bit_length(), None,
                                ALU.logical_shift_right)
                v.tensor_scalar(place_i[:, :], edge_i[:, 0, :], L - 1, None, ALU.bitwise_and)
                link(dve, v.tensor_tensor(count[:, 0:NPP], end, first, ALU.subtract))
                v.tensor_scalar(rcount[:, :], count[:, 0:NPP], 1.0, None, ALU.max)
                v.tensor_scalar(some[:, 0:NPP], count[:, 0:NPP], 0.0, None, ALU.is_gt)
                v.tensor_scalar(mark[:, :], place_i[:, :], 1.0, None, ALU.add)
                link(dve, v.tensor_copy(chunk_f[:, :, :], chunk_i[:, :, :]))
                for j in range(2):
                    last = v.tensor_tensor(slot_f[:, j, :], chunk_f[:, j, :], nodef[:, 0:NPP], ALU.add)
                link(dve, last)
                link(dve, v.tensor_copy(slot_i[:, :, :], slot_f[:, :, :]))
                v.tensor_scalar(tile_i[:, :], slot_i[:, 0, :], 7, None, ALU.logical_shift_right)
                link(dve, v.tensor_scalar(lane_i[:, :], slot_i[:, 0, :], P - 1, None, ALU.bitwise_and))
                v.tensor_copy(tile_f[:, :], tile_i[:, :])
                link(dve, v.tensor_copy(lane_f[:, :], lane_i[:, :]))

                def one_hots(i, k):
                    b = bass.ds(U * i + k, 1)
                    at_least(dve, hot_used, U * i + k - U + 1)
                    v.tensor_scalar(lane_hot[:, k, :], iotab[:, 0:P], lane_f[:, b], None, ALU.is_equal)
                    v.tensor_scalar(tile_hot[:, k, :], iotab[:, 0:T], tile_f[:, b], mark[:, b], ALU.is_equal,
                                    ALU.mult).then_inc(hot_done, 1)
                rolled(dve, NPP, [(one_hots, 0)])
                dve.wait_ge(hot_used, NPP)
                v.tensor_scalar(starts[:, :], ps_mask[:, 0:T], 0.0, None, ALU.is_gt).then_inc(starts_done, 1)
                v.tensor_scalar(before[:, 0:T], ps_mask[:, 0:T], -1.0, 0.0, ALU.add, ALU.max).then_inc(before_done, 1)
                dve.wait_ge(starts_done, 1)
                v.tensor_scalar(goes_on[:, :], starts[:, :], -1.0, 1.0, ALU.mult, ALU.add).then_inc(goes_on_done, 1)
                v.reciprocal(rcount[:, :], rcount[:, :])
                link(dve, v.tensor_tensor(slots_l[:, :], slot_f[:, 1, :], slot_f[:, 0, :], ALU.subtract))
                link(dve, v.tensor_scalar(slots_l[:, :], slots_l[:, :], 1.0, float(L), ALU.add, ALU.mult))
                link(dve, v.tensor_tensor(slots_l[:, :], slots_l[:, :], some[:, 0:NPP], ALU.mult))
                v.tensor_tensor(others[:, :], slots_l[:, :], count[:, 0:NPP], ALU.subtract)
                dve.wait_ge(next_before, 1)
                link(dve, v.tensor_scalar(kept[:, :], ps_z[0][:, 0:T], 0.0, float(L), ALU.is_equal, ALU.mult))
                link(dve, v.tensor_tensor(kept[:, :], kept[:, :], ps_z[0][:, 0:T], ALU.add))
                for l in range(L):
                    v.tensor_scalar(late[:, :, l], kept[:, :], float(l), None, ALU.is_le)
                dve.wait_ge(prefix_done, 1)
                link(dve, v.tensor_copy(total[:, :], ps_r[:, 256:256 + T]))
                link(dve, v.tensor_tensor_scan(out=upto[:, :], data0=total[:, :], data1=zeros[:, :],
                                               initial=-1.0, op0=ALU.add, op1=ALU.add))
                link(dve, v.tensor_tensor(upto[:, :], upto[:, :], total[:, :], ALU.subtract))
                v.tensor_tensor(s_node[:, :], upto[:, :], ps_r[:, 0:T], ALU.add).then_inc(s_node_done, 1)
                for l in range(L):
                    last = v.scalar_tensor_tensor(inv[:, :, l], before[:, 0:T], float(l), late[:, :, l], ALU.is_gt,
                                                  ALU.add)
                last.then_inc(inv_done, 1)
                for g, (t0, n) in enumerate(TILE_GROUPS):
                    turned_ = ps_z[1][0:n, g * P:(g + 1) * P]
                    dve.wait_ge(nodes_turned, g + 1)
                    if g == 0:
                        dve.wait_ge(nodes_turned, 2)
                    v.tensor_scalar(first_node[0:n, g:g + 1], turned_[:, 0:1], float(NPP * P - P), None,
                                    ALU.min).then_inc(first_done, 1)
                    dve.wait_ge(first_done, g + 1)
                    v.tensor_scalar(nrows[0:n, g, :], turned_, first_node[0:n, g:g + 1], None,
                                    ALU.subtract).then_inc(nrows_done, 1)
                link(dve, v.tensor_tensor(upto[:, :], slotf[:, :], s_node[:, :], ALU.subtract))
                v.tensor_scalar(s_index[:, :], upto[:, :], float(CHUNKS - 1), None, ALU.min)
                dve.wait_ge(inv_done, 1)
                v.tensor_scalar(base_i[:, :], s_node[0:1, :], float(NPP * P - P), None, ALU.min)
                v.tensor_scalar(own[:, :, :], inv[:, :, :], -1.0, 1.0, ALU.mult, ALU.add)

        stage.close()
        idx = ring("idx", [P, U, 1], I32)
        ea = ring("ea", [P, U, L * FE])
        uw = ring("uw", [P, U, F])
        sel = ring("sel", [P, U, P])
        eaT = ring("eaT", [P, U, L // 2, P])
        nuT = ring("nuT", [P, U, P])
        rp = ring("rp", [P, U, L, P])
        half = ring("half", [P, U, 2, P])
        rsum = ring("rsum", [P, U, P])
        mred = ring("mred", [P, U, P])
        smax = ring("smax", [P, U, P])
        ssum = ring("ssum", [P, U, P])
        rT = ring("rT", [P, U, 2 * P])
        masks = ring("masks", [P, U, ROW], U8)
        near = ring("near", [P, U, P], BF16)
        near_in = [sem(f"near_in{k}") for k in range(U // 2)]
        masks_in = [sem(f"masks_in{k}") for k in range(U // 2)]
        ea_in = [sem(f"ea_in{k}") for k in range(U)]
        uw_in = [sem(f"uw_in{k}") for k in range(U)]
        rows_out = [sem(f"rows_out{k}") for k in range(U // 2)]
        idx_done = sem("idx_done")
        ea_done = sem("ea_done")
        opened = sem("opened")
        seeded = sem("seeded")
        turned = sem("turned")
        eaT_done = sem("eaT_done")
        z_done = sem("z_done")
        rp_done = sem("rp_done")
        half_done = sem("half_done")
        rsum_done = sem("rsum_done")
        m_done = sem("m_done")
        sel_done = sem("sel_done")
        mred_done = sem("mred_done")
        scan_done = sem("scan_done")
        prepared = sem("prepared")
        r_turned = sem("r_turned")
        rT_done = sem("rT_done")


        with nc.Block() as block:
            @block.gpsimd
            def _(pool):
                def take_index(i, k):
                    t = U * i + k
                    if not (isinstance(i, int) and i == 0):
                        pool.wait_ge(ea_in[k], 16 * i)
                    nc.gpsimd.tensor_copy(idx[:, k, :], s_index[:, bass.ds(t, 1)]).then_inc(idx_done, 1)

                def gather(i, k):
                    t = U * i + k
                    at_least(pool, idx_done, t + 1)
                    at_least(pool, turned, t - U + 1, alone=True)
                    pool.indirect_dma_start(
                        out=ea[:, k, :], out_offset=None, in_=chunk_rows,
                        in_offset=bass.IndirectOffsetOnAxis(ap=idx[:, k, :], axis=0)
                    ).then_inc(ea_in[k], 16)

                def add_halves(i, k):
                    t = U * i + k
                    at_least(pool, rp_done, t + 1)
                    at_least(pool, rsum_done, t - U + 1)
                    nc.gpsimd.tensor_tensor(half[:, k, :, :], rp[:, k, 0:2, :], rp[:, k, 2:4, :],
                                            ALU.add).then_inc(half_done, 1)

                def sum_edges(i, k):
                    t = U * i + k
                    at_least(pool, half_done, t + 1)
                    at_least(pool, scan_done, t - U + 1)
                    nc.gpsimd.tensor_tensor(rsum[:, k, :], half[:, k, 0, :], half[:, k, 1, :],
                                            ALU.add).then_inc(rsum_done, 1)
                rolled(pool, T, [(add_halves, 0), (gather, 5), (sum_edges, 0), (take_index, 6)])

            @block.tensor
            def _(pe):
                def turn(i, k):
                    t = U * i + k
                    at_least(pe, ea_done, t + 1)
                    pe.wait_ge(uw_in[k], 16 * i + 16)
                    at_least(pe, sel_done, t + 1)
                    at_least(pe, eaT_done, t - 1)
                    nc.tensor.transpose(ps_t[k % 2][:, 0:P], ea[:, k, 0:P], ident[:, :])
                    nc.tensor.transpose(ps_t[k % 2][:, P:2 * P], ea[:, k, P:2 * P], ident[:, :])
                    nc.tensor.matmul(ps_t[k % 2][:, 2 * P:3 * P], uw[:, k, :], sel[:, k, :], start=True,
                                     stop=True).then_inc(turned, 1)

                def edge_product(i, k):
                    t = U * i + k
                    at_least(pe, eaT_done, t + 1)
                    at_least(pe, rp_done, t - 1)
                    z = ps_z[k % 2].rearrange("f (j r s) -> f j r s", j=L // 2, r=2)
                    for r in range(2):
                        last = nc.tensor.matmul(z[:, :, r, :], w1b[:, r, :], eaT[:, k, :, :], start=True, stop=True)
                    last.then_inc(z_done, 1)

                def message(i, k):
                    t = U * i + k
                    at_least(pe, rp_done, t + 1)
                    at_least(pe, seeded, t + 1)
                    nc.tensor.matmul(ps_m[k % 2][:, :], w2[:, :], rp[:, k, :, :], start=False, stop=True,
                                     skip_group_check=True).then_inc(m_done, 1)

                def turn_scans(i, k):
                    t = U * i + k
                    at_least(pe, scan_done, t + 1)
                    at_least(pe, rT_done, t)
                    nc.tensor.transpose(ps_r[:, 0:P], smax[:, k, :], ident[:, :])
                    nc.tensor.transpose(ps_r[:, P:2 * P], ssum[:, k, :], ident[:, :]).then_inc(r_turned, 1)
                for m in ps_m:
                    for l in range(L):
                        last = nc.tensor.matmul(m[:, l * P:(l + 1) * P], identb[:, :], identb[:, :], start=l == 0,
                                                stop=True, skip_group_check=True)
                last.then_inc(opened, 1)
                rolled(pe, T, [(turn, 1), (edge_product, 0), (message, -1), (turn_scans, -3)])

            @block.scalar
            def _(act):
                def zero_others(i, k):
                    t = U * i + k
                    act.wait_ge(ea_in[k], 16 * i + 16)
                    for l in range(L):
                        last = nc.scalar.activation(ea[:, k, l * FE:(l + 1) * FE], ea[:, k, l * FE:(l + 1) * FE],
                                                    ACT.Copy, scale=own[:, bass.ds(t, 1), l])
                    last.then_inc(ea_done, 1)

                def take_turned(i, k):
                    t = U * i + k
                    at_least(act, turned, t + 1)
                    at_least(act, z_done, t - U + 1)
                    at_least(act, rp_done, t - U + 1)
                    nc.scalar.activation(eaT[:, k, :, :], ps_t[k % 2][:, 0:2 * P], ACT.Copy)
                    nc.scalar.activation(nuT[:, k, :], ps_t[k % 2][:, 2 * P:3 * P], ACT.Copy,
                                         scale=-1.0).then_inc(eaT_done, 1)

                def seed(i, k):
                    t = U * i + k
                    if isinstance(t, int) and t == 0:
                        act.wait_ge(opened, 1)
                    act.wait_ge(masks_in[k // 2], 16 * i + 16)
                    at_least(act, mred_done, t - 1)
                    nc.scalar.activation(ps_m[k % 2][:, :], masks[:, k, MASKS:ROW], ACT.Copy,
                                         scale=-BIG).then_inc(seeded, 1)

                def take_rows(i, k):
                    t = U * i + k
                    at_least(act, r_turned, t + 1)
                    at_least(act, rows_out[k // 2], 16 * i)
                    nc.scalar.activation(rT[:, k, :], ps_r[:, 0:2 * P], ACT.Copy).then_inc(rT_done, 1)
                rolled(act, T, [(seed, -1), (take_rows, -4), (take_turned, 1), (zero_others, 3)])

            @block.sync
            def _(sp):
                def load_u(i, k):
                    t = U * i + k
                    at_least(sp, turned, t - U + 1)
                    first = sp.value_load(base_i[0:1, bass.ds(t, 1)], min_val=0, max_val=NPP * P - P)
                    sp.dma_start(uw[:, k, :], utab[bass.ds(first, P), :]).then_inc(uw_in[k], 16)

                sp.wait_ge(ntab_out, 32)
                sp.wait_ge(mtab_out, 32)

                def load_near(i, k):
                    if k % 2:
                        return
                    t = U * i + k
                    n = min(2, T - t) if isinstance(t, int) else 2
                    at_least(sp, sel_done, t + n - U)
                    sp.dma_start(near[:, k:k + n, :],
                                 ntab[bass.ds(t, n), :].rearrange("(a t) f -> a t f", a=1).broadcast_to([P, n, P])
                                 ).then_inc(near_in[k // 2], 16)

                def load_masks(i, k):
                    if k % 2:
                        return
                    t = U * i + k
                    n = min(2, T - t) if isinstance(t, int) else 2
                    at_least(sp, scan_done, t + n - U, alone=True)
                    sp.dma_start(masks[:, k:k + n, :],
                                 mtab[bass.ds(t, n), :].rearrange("(a t) f -> a t f", a=1).broadcast_to([P, n, ROW])
                                 ).then_inc(masks_in[k // 2], 16)

                def store(i, k):
                    t = U * i + k
                    alone = isinstance(t, int) and t == T - 1 and k % 2 == 0
                    if k % 2 == 0 and not alone:
                        return
                    n = 1 if alone else 2
                    at_least(sp, rT_done, t + 1)
                    sp.dma_start(rtab[bass.ds((t + 1 - n) * P, n * P), :].rearrange("(t p) f -> p t f", p=P),
                                 rT[:, k + 1 - n:k + 1, :]).then_inc(rows_out[k // 2], 16)
                rolled(sp, T, [(load_near, 4), (load_u, 3), (load_masks, 1), (store, -4)])
                for h in range(U // 2):
                    sp.wait_ge(rows_out[h], 16 * ((T - 2 * h + U - 1) // U))

            @block.vector
            def _(dve):
                v = nc.vector

                def select_nodes(i, k):
                    t = U * i + k
                    dve.wait_ge(near_in[k // 2], 16 * i + 16)
                    at_least(dve, turned, t - U + 1)
                    v.tensor_scalar(sel[:, k, :], near[:, k, :], row[:, :], None,
                                    ALU.is_equal).then_inc(sel_done, 1)

                def relu_less_u(i, k):
                    t = U * i + k
                    at_least(dve, z_done, t + 1)
                    at_least(dve, m_done, t - U + 1)
                    at_least(dve, rsum_done, t - U + 1)
                    v.tensor_tensor(rp[:, k, :, :], ps_z[k % 2].rearrange("f (l s) -> f l s", l=L),
                                    nuT[:, k:k + 1, :].broadcast_to([P, L, P]), ALU.max).then_inc(rp_done, 1)

                def reduce_message(i, k):
                    t = U * i + k
                    at_least(dve, m_done, t + 1)
                    at_least(dve, scan_done, t - U + 1)
                    v.tensor_reduce(mred[:, k, :], ps_m[k % 2].rearrange("f (l s) -> f s l", l=L), AX.X,
                                    ALU.max).then_inc(mred_done, 1)

                def scan(i, k):
                    t = U * i + k
                    at_least(dve, rsum_done, t + 1)
                    dve.wait_ge(masks_in[k // 2], 16 * i + 16)
                    at_least(dve, mred_done, t + 1)
                    at_least(dve, scan_done, t)
                    at_least(dve, r_turned, t - U + 1)
                    first, before = isinstance(t, int) and t == 0, (k - 1) % U
                    v.tensor_tensor_scan(out=ssum[:, k, :], data0=masks[:, k, 2 * P:MASKS].bitcast(BF16), data1=rsum[:, k, :],
                                         initial=0.0 if first else ssum[:, before, P - 1:P], op0=ALU.mult,
                                         op1=ALU.add)
                    v.tensor_tensor_scan(out=smax[:, k, :], data0=masks[:, k, 0:2 * P].bitcast(BF16), data1=mred[:, k, :],
                                         initial=-BIG if first else smax[:, before, P - 1:P], op0=ALU.add,
                                         op1=ALU.max).then_inc(scan_done, 1)
                def prepare(i, k):
                    if isinstance(i, int) and i >= PREP or k == 0:
                        return
                    b = bass.ds(i, 1)
                    at_least(dve, prepared, 3 * i + k - 1)
                    if k == 1:
                        v.tensor_tensor(xs[:, b, :], xs[:, b, :], bor[:, 0:1, :], ALU.add).then_inc(prepared, 1)
                    elif k == 2:
                        v.scalar_tensor_tensor(xs[:, b, :], uv[:, b, 1, :], some[:, b], xs[:, b, :], ALU.mult,
                                               ALU.add).then_inc(prepared, 1)
                    else:
                        v.scalar_tensor_tensor(xs[:, b, :], b2s[:, :, :], count[:, b], xs[:, b, :], ALU.mult,
                                               ALU.add).then_inc(prepared, 1)
                rolled(dve, T, [(select_nodes, 2), (prepare, 0), (scan, -2), (relu_less_u, 0), (reduce_message, -1)])

        stage.close()
        rg = ring("rg", [P, NPP, 2 * F])
        ru = ring("ru", [P, U, F])
        sm = ring("sm", [P, U, 2 * F])
        smT = ring("smT", [P, U, 2, P])
        ob = ring("ob", [P, U, F])
        rg_in = [sem(f"rg_in{k}") for k in range(U)]
        ru_done = sem("ru_done")
        own_done = sem("own_done")
        sum_mid = sem("sum_mid")
        sum_done = sem("sum_done")
        sm_turned = sem("sm_turned")
        smT_done = sem("smT_done")
        o_done = sem("o_done")
        o_mid = sem("o_mid")
        o_ready = sem("o_ready")
        out_out = sem("out_out")
        ps_s, ps_o = bank[0:2], bank[2:4]

        with nc.Block() as block:
            @block.gpsimd
            def _(pool):
                for b in range(NPP):
                    if b >= U:
                        pool.wait_ge(rg_in[b % U], 16 * (b // U))
                    pool.indirect_dma_start(
                        out=rg[:, b, :], out_offset=None, in_=rtab,
                        in_offset=bass.IndirectOffsetOnAxis(ap=slot_i[:, 1, b:b + 1], axis=0)
                    ).then_inc(rg_in[b % U], 16)

            @block.scalar
            def _(act):
                def others_relu(i, k):
                    b = U * i + k
                    at_least(act, sum_done, b - U + 1)
                    nc.scalar.activation(ru[:, k, :], uv[:, bass.ds(b, 1), 0, :], ACT.Relu,
                                         scale=others[:, bass.ds(b, 1)]).then_inc(ru_done, 1)

                def drop_empty(i, k):
                    b = U * i + k
                    act.wait_ge(rg_in[k], 16 * i + 16)
                    at_least(act, sm_turned, b - U + 1)
                    nc.scalar.activation(sm[:, k, :], rg[:, bass.ds(b, 1), :], ACT.Copy,
                                         scale=some[:, bass.ds(b, 1)]).then_inc(own_done, 1)

                def take_turned(i, k):
                    b = U * i + k
                    at_least(act, sm_turned, b + 1)
                    at_least(act, o_done, b - U + 1)
                    nc.scalar.activation(smT[:, k, :, :], ps_s[k % 2][:, 0:2 * P], ACT.Copy).then_inc(smT_done, 1)
                rolled(act, NPP, [(others_relu, 3), (drop_empty, 3), (take_turned, 0)])

            @block.tensor
            def _(pe):
                def turn(i, k):
                    b = U * i + k
                    at_least(pe, sum_done, b + 1)
                    at_least(pe, smT_done, b - 1)
                    nc.tensor.transpose(ps_s[k % 2][:, 0:P], sm[:, k, F:2 * F], ident[:, :])
                    nc.tensor.transpose(ps_s[k % 2][:, P:2 * P], sm[:, k, 0:F], ident[:, :]).then_inc(sm_turned, 1)

                def outputs(i, k):
                    b = U * i + k
                    at_least(pe, smT_done, b + 1)
                    at_least(pe, o_ready, b - 1)
                    nc.tensor.matmul(ps_o[k % 2][:, 0:2 * F], smT[:, k, 0, :], w2o[:, 0:2, :], start=True, stop=False,
                                     skip_group_check=True)
                    nc.tensor.matmul(ps_o[k % 2][:, 0:F], smT[:, k, 1, :], wo[:, 2, :], start=False, stop=True,
                                     skip_group_check=True).then_inc(o_done, 1)
                rolled(pe, NPP, [(turn, 1), (outputs, 0)])

            @block.vector
            def _(dve):
                v = nc.vector

                def sum_relu(i, k):
                    b = U * i + k
                    at_least(dve, own_done, b + 1)
                    v.scalar_tensor_tensor(sm[:, k, F:2 * F], uv[:, bass.ds(b, 1), 0, :], slots_l[:, bass.ds(b, 1)],
                                           sm[:, k, F:2 * F], ALU.mult, ALU.add).then_inc(sum_mid, 1)

                def less_others(i, k):
                    b = U * i + k
                    at_least(dve, sum_mid, b + 1)
                    at_least(dve, ru_done, b + 1)
                    v.tensor_tensor(sm[:, k, F:2 * F], sm[:, k, F:2 * F], ru[:, k, :], ALU.subtract).then_inc(sum_done, 1)

                def add_mean(i, k):
                    b = U * i + k
                    at_least(dve, o_done, b + 1)
                    v.scalar_tensor_tensor(ob[:, k, :], ps_o[k % 2][:, F:2 * F], rcount[:, bass.ds(b, 1)],
                                           xs[:, bass.ds(b, 1), :], ALU.mult, ALU.add).then_inc(o_mid, 1)

                def add_rest(i, k):
                    b = U * i + k
                    at_least(dve, o_mid, b + 1)
                    v.tensor_tensor(xs[:, bass.ds(b, 1), :], ob[:, k, :], ps_o[k % 2][:, 0:F],
                                    ALU.add).then_inc(o_ready, 1)
                rolled(dve, NPP, [(sum_relu, 2), (add_mean, -1), (less_others, 2), (add_rest, -1)])

            @block.sync
            def _(sp):
                LATE = NPP - (NPP - REST) // 4
                stored = 0
                for b0, b1_ in ((0, REST), (REST, LATE), (LATE, NPP)):
                    sp.wait_ge(o_ready, b1_)
                    for p0, p1, nb, rows in node_rows(out):
                        if nb > b0:
                            sp.dma_start(rows[:, b0:b1_, :], xs[p0:p1, b0:b1_, :]).then_inc(out_out, 16)
                            stored += 1
                sp.wait_ge(out_out, 16 * stored)


_INS = ["x", "dst", "edge_attr_64", "L0_gnn_W1", "L0_gnn_b1", "L0_gnn_W2", "L0_gnn_b2", "L0_gnn_Wm", "L0_gnn_bm",
        "L0_gnn_Wx", "L0_gnn_bx", "L0_gnn_Ws", "L0_gnn_bs"]


def kernel(**inputs):
    import numpy as np

    import concourse.bacc as bacc
    from concourse.bass_utils import run_bass_kernel_spmd

    nc = bacc.Bacc("TRN2", target_bir_lowering=False, num_devices=1)
    arrays, args = {}, []
    for name in _INS:
        a = np.ascontiguousarray(inputs[name])
        arrays[f"in_{name}"] = a
        args.append(nc.dram_tensor(f"in_{name}", a.shape, mybir.dt.from_np(a.dtype), kind="ExternalInput").ap())
    args.append(nc.dram_tensor("out_0", inputs["x"].shape, F32, kind="ExternalOutput").ap())
    gnn_kernel(nc, *args)
    r = run_bass_kernel_spmd(nc, [arrays], core_ids=[0])
    return r.results[0]["out_0"]
```
